# Optimizing a Trainium2 kernel written in Bass

```python
import numpy as np
import jax
import jax.numpy as jnp

def _softmax(x, axis=-1):
    return jax.nn.softmax(x, axis=axis)

def _gelu(x):
    return jax.nn.gelu(x, approximate=True)

def _silu(x):
    return jax.nn.silu(x)

def _sigmoid(x):
    return jax.nn.sigmoid(x)

def _layernorm(x, axis=-1, eps=1e-05):
    m = jnp.mean(x, axis=axis, keepdims=True)
    v = jnp.var(x, axis=axis, keepdims=True)
    return (x - m) / jnp.sqrt(v + eps)

def _scatter_add(tgt, idx, src, axis=0):
    return tgt.at[idx].add(src)

def _segment_sum(src, seg, n):
    return jax.ops.segment_sum(src, seg, n)
kernel_name = 'mk_decoder_postln_d2_seqx_r8_db3805'

def setup_inputs(seed: int=0):
    np.random.seed(seed)
    _w = jnp.asarray

    def _rec_inputs():
        import jax
        import jax.numpy as jnp
        _rk = jax.random.key(seed)
        x = -0.0005207 + 1.001 * jax.random.normal(jax.random.fold_in(_rk, 1), (64, 64, 128), jnp.float32)
        _lenS = 64 - jax.random.randint(jax.random.fold_in(_rk, 7), (64,), 0, max(1, 64 // 4) + 1, jnp.int32)
        _lenS2 = 64 - jax.random.randint(jax.random.fold_in(_rk, 8), (64,), 0, max(1, 64 // 4) + 1, jnp.int32)
        _ctx_512P = jax.random.normal(jax.random.fold_in(_rk, 11), (64, 16, 64), jnp.float32)
        _ctx_512c = jax.random.dirichlet(jax.random.fold_in(_rk, 511), 0.3 * jnp.ones((16,), jnp.float32), (64, 64))
        _ctx_512t = jnp.einsum('bsk,bkd->bsd', _ctx_512c, _ctx_512P)
        _ctx_512t = _ctx_512t * jax.lax.rsqrt(jnp.mean(jnp.square(_ctx_512t)) + 1e-12) * 0.953939
        ctx_512 = 0.502058 + 0.29099 * (_ctx_512t + 0.3 * jax.random.normal(jax.random.fold_in(_rk, 611), (64, 64, 64), jnp.float32))
        itok_BxS2xS_0_7 = jax.random.randint(jax.random.fold_in(_rk, 12), (64, 64, 64), 0, 8, jnp.int32)
        return (x, ctx_512, itok_BxS2xS_0_7)
    x, ctx_512, itok_BxS2xS_0_7 = _rec_inputs()

    def _L0_attn_setup():
        import jax, jax.numpy as jnp
        import numpy as np
        D = 128
        H = 16
        key = jax.random.key(seed)
        ks = jax.random.split(key, 5)
        x = jax.random.normal(ks[0], (2, 256, D), dtype=jnp.float32)
        s = 0.02
        W_attn = jax.random.normal(ks[1], (D, 3 * D), dtype=jnp.float32) * s
        b_attn = jnp.zeros((3 * D,), dtype=jnp.float32)
        W_proj = jax.random.normal(ks[2], (D, D), dtype=jnp.float32) * s
        b_proj = jnp.zeros((D,), dtype=jnp.float32)
        return {'x': x, 'W_attn': W_attn, 'b_attn': b_attn, 'W_proj': W_proj, 'b_proj': b_proj}
    _L0_attn_all = _L0_attn_setup()
    _L0_attn_in = {k: v for k, v in _L0_attn_all.items() if k in ('W_attn', 'b_attn', 'W_proj', 'b_proj')}
    del _L0_attn_all

    def _L0_xattn_setup():
        import jax, jax.numpy as jnp
        import numpy as np
        key = jax.random.key(seed)
        k1, k2, k3, k4, k5 = jax.random.split(key, 5)
        B, K, S, E, I, D = (4, 2, 64, 8, 128, 256)
        x = jax.random.normal(k1, (B, S, I), dtype=jnp.float32)
        weights = jax.random.uniform(k2, (B, K, S), dtype=jnp.float32)
        ensembles = jax.random.randint(k3, (B, K, S), 0, E, dtype=jnp.int64)
        lim1 = float(np.sqrt(6.0 / (D + I)))
        proj_in = jax.random.uniform(k4, (E, D, I), dtype=jnp.float32, minval=-lim1, maxval=lim1)
        proj_out = jax.random.uniform(k5, (E, I, D), dtype=jnp.float32, minval=-lim1, maxval=lim1)
        return {'x': x, 'weights': weights, 'ensembles': ensembles, 'proj_in': proj_in, 'proj_out': proj_out}
    _L0_xattn_all = _L0_xattn_setup()
    _L0_xattn_in = {k: v for k, v in _L0_xattn_all.items() if k in ('proj_in', 'proj_out')}
    del _L0_xattn_all

    def _L0_ffn_setup():
        import jax, jax.numpy as jnp
        import numpy as np
        D_MODEL = 128
        N_EXPERTS = 8
        TOP_K = 2
        key = jax.random.key(seed)
        ks = jax.random.split(key, 8)
        d, e = (D_MODEL, N_EXPERTS)
        s = 1.0 / np.sqrt(d)
        return {'x': jax.random.normal(ks[0], (4, 256, d), dtype=jnp.float32), 'W_gate': jax.random.uniform(ks[1], (d, e), jnp.float32, -s, s), 'b_gate': jax.random.uniform(ks[2], (e,), jnp.float32, -s, s), 'W1': jax.random.uniform(ks[3], (e, d, d), jnp.float32, -s, s), 'b1': jax.random.uniform(ks[4], (e, d), jnp.float32, -s, s), 'W2': jax.random.uniform(ks[5], (e, d, d), jnp.float32, -s, s), 'b2': jax.random.uniform(ks[6], (e, d), jnp.float32, -s, s)}
    _L0_ffn_all = _L0_ffn_setup()
    _L0_ffn_in = {k: v for k, v in _L0_ffn_all.items() if k in ('W_gate', 'b_gate', 'W1', 'b1', 'W2', 'b2')}
    del _L0_ffn_all

    def _L1_attn_setup():
        import jax, jax.numpy as jnp
        import numpy as np
        key = jax.random.key(seed)
        x = jax.random.normal(key, (8, 512, 128), dtype=jnp.float32)
        return {'x': x}
    _L1_attn_all = _L1_attn_setup()
    _L1_attn_in = {k: v for k, v in _L1_attn_all.items() if k in ()}
    del _L1_attn_all

    def _L1_xattn_setup():
        import jax, jax.numpy as jnp
        import numpy as np
        B, LQ, LK = (8, 256, 256)
        QD, KD, VD = (128, 64, 64)
        key = jax.random.key(seed)
        ks = jax.random.split(key, 9)
        s = 0.02
        return {'query': jax.random.normal(ks[0], (B, LQ, QD), jnp.float32), 'key': jax.random.normal(ks[1], (B, LK, KD), jnp.float32), 'value': jax.random.normal(ks[2], (B, LK, VD), jnp.float32), 'Wq': jax.random.normal(ks[3], (QD, QD), jnp.float32) * s, 'bq': jnp.zeros((QD,), jnp.float32), 'Wk': jax.random.normal(ks[4], (KD, QD), jnp.float32) * s, 'bk': jnp.zeros((QD,), jnp.float32), 'Wv': jax.random.normal(ks[5], (VD, QD), jnp.float32) * s, 'bv': jnp.zeros((QD,), jnp.float32)}
    _L1_xattn_all = _L1_xattn_setup()
    _L1_xattn_in = {k: v for k, v in _L1_xattn_all.items() if k in ('Wq', 'bq', 'Wk', 'bk', 'Wv', 'bv')}
    del _L1_xattn_all

    def _L1_ffn_setup():
        import jax, jax.numpy as jnp
        import numpy as np
        N_EMBD = 128
        NUM_EXPERTS = 8
        TOP_K = 2
        D_FF = 4 * N_EMBD
        B, S = (4, 256)
        key = jax.random.key(seed)
        ks = jax.random.split(key, 7)
        scale = lambda fan_in: 1.0 / np.sqrt(fan_in)
        x = jax.random.normal(ks[0], (B, S, N_EMBD), dtype=jnp.float32)
        W_router = jax.random.normal(ks[1], (N_EMBD, NUM_EXPERTS), dtype=jnp.float32) * scale(N_EMBD)
        b_router = jnp.zeros((NUM_EXPERTS,), dtype=jnp.float32)
        W1 = jax.random.normal(ks[2], (NUM_EXPERTS, N_EMBD, D_FF), dtype=jnp.float32) * scale(N_EMBD)
        b1 = jnp.zeros((NUM_EXPERTS, D_FF), dtype=jnp.float32)
        W2 = jax.random.normal(ks[3], (NUM_EXPERTS, D_FF, N_EMBD), dtype=jnp.float32) * scale(D_FF)
        b2 = jnpp = jnp.zeros((NUM_EXPERTS, N_EMBD), dtype=jnp.float32)
        return {'x': x, 'W_router': W_router, 'b_router': b_router, 'W1': W1, 'b1': b1, 'W2': W2, 'b2': b2}
    _L1_ffn_all = _L1_ffn_setup()
    _L1_ffn_in = {k: v for k, v in _L1_ffn_all.items() if k in ('W_router', 'b_router', 'W1', 'b1', 'W2', 'b2')}
    del _L1_ffn_all
    return {'x': x, 'ctx_512': ctx_512, 'itok_BxS2xS_0_7': itok_BxS2xS_0_7, 'L0_attn_W_attn': _L0_attn_in['W_attn'], 'L0_attn_b_attn': _L0_attn_in['b_attn'], 'L0_attn_W_proj': _L0_attn_in['W_proj'], 'L0_attn_b_proj': _L0_attn_in['b_proj'], 'L0_xattn_proj_in': _L0_xattn_in['proj_in'], 'L0_xattn_proj_out': _L0_xattn_in['proj_out'], 'L0_ffn_W_gate': _L0_ffn_in['W_gate'], 'L0_ffn_b_gate': _L0_ffn_in['b_gate'], 'L0_ffn_W1': _L0_ffn_in['W1'], 'L0_ffn_b1': _L0_ffn_in['b1'], 'L0_ffn_W2': _L0_ffn_in['W2'], 'L0_ffn_b2': _L0_ffn_in['b2'], 'L1_xattn_Wq': _L1_xattn_in['Wq'], 'L1_xattn_bq': _L1_xattn_in['bq'], 'L1_xattn_Wk': _L1_xattn_in['Wk'], 'L1_xattn_bk': _L1_xattn_in['bk'], 'L1_xattn_Wv': _L1_xattn_in['Wv'], 'L1_xattn_bv': _L1_xattn_in['bv'], 'L1_ffn_W_router': _L1_ffn_in['W_router'], 'L1_ffn_b_router': _L1_ffn_in['b_router'], 'L1_ffn_W1': _L1_ffn_in['W1'], 'L1_ffn_b1': _L1_ffn_in['b1'], 'L1_ffn_W2': _L1_ffn_in['W2'], 'L1_ffn_b2': _L1_ffn_in['b2']}

def reference(x, ctx_512, itok_BxS2xS_0_7, L0_attn_W_attn, L0_attn_b_attn, L0_attn_W_proj, L0_attn_b_proj, L0_xattn_proj_in, L0_xattn_proj_out, L0_ffn_W_gate, L0_ffn_b_gate, L0_ffn_W1, L0_ffn_b1, L0_ffn_W2, L0_ffn_b2, L1_xattn_Wq, L1_xattn_bq, L1_xattn_Wk, L1_xattn_bk, L1_xattn_Wv, L1_xattn_bv, L1_ffn_W_router, L1_ffn_b_router, L1_ffn_W1, L1_ffn_b1, L1_ffn_W2, L1_ffn_b2):
    import jax
    import jax.numpy as jnp

    def _L0_attn_ref(x, W_attn, b_attn, W_proj, b_proj):
        import jax, jax.numpy as jnp
        import numpy as np
        D = 128
        H = 16
        B, S, E = x.shape
        hd = E // H
        qkv = x @ W_attn + b_attn
        q, k, v = jnp.split(qkv, 3, axis=-1)
        q = q.reshape(B, S, H, hd).transpose(0, 2, 1, 3)
        k = k.reshape(B, S, H, hd).transpose(0, 2, 1, 3)
        v = v.reshape(B, S, H, hd).transpose(0, 2, 1, 3)
        att = jnp.einsum('bhqd,bhkd->bhqk', q, k) * (1.0 / jnp.sqrt(jnp.float32(hd)))
        causal = jnp.tril(jnp.ones((S, S), dtype=bool))
        att = jnp.where(causal, att, -jnp.inf)
        att = jax.nn.softmax(att, axis=-1)
        y = jnp.einsum('bhqk,bhkd->bhqd', att, v)
        y = y.transpose(0, 2, 1, 3).reshape(B, S, E)
        return y @ W_proj + b_proj

    def _L0_xattn_ref(x, weights, ensembles, proj_in, proj_out):
        import jax, jax.numpy as jnp
        import numpy as np
        E = proj_in.shape[0]
        h = jax.nn.relu(jnp.einsum('edi,bsi->bsed', proj_in, x))
        o = jnp.einsum('eid,bsed->bsei', proj_out, h)
        onehot = jax.nn.one_hot(ensembles, E, dtype=x.dtype)
        gate = jnp.einsum('bks,bkse->bse', weights, onehot)
        return jnp.einsum('bsei,bse->bsi', o, gate)

    def _L0_ffn_ref(x, W_gate, b_gate, W1, b1, W2, b2):
        import jax, jax.numpy as jnp
        import numpy as np
        D_MODEL = 128
        N_EXPERTS = 8
        TOP_K = 2
        B, T, d = x.shape
        xf = x.reshape(-1, d)
        scores = xf @ W_gate + b_gate
        topk_val, topk_idx = jax.lax.top_k(scores, TOP_K)
        onehot = jax.nn.one_hot(topk_idx, N_EXPERTS, dtype=xf.dtype)
        w = jnp.einsum('nk,nke->ne', topk_val, onehot)
        h = jax.nn.relu(jnp.einsum('nd,edh->neh', xf, W1) + b1)
        y = jnp.einsum('neh,ehd->ned', h, W2) + b2
        out = jnp.einsum('ned,ne->nd', y, w)
        return out.reshape(B, T, d)

    def _L1_attn_ref(x):
        import jax, jax.numpy as jnp
        import numpy as np
        B, T, C = x.shape
        tril = jnp.tril(jnp.ones((T, T), dtype=jnp.float32))
        attn = jnp.where(tril == 0, -jnp.inf, jnp.zeros((T, T), dtype=jnp.float32))
        attn = jax.nn.softmax(attn, axis=-1)
        return jnp.einsum('ts,bsc->btc', attn, x)

    def _L1_xattn_ref(query, key, value, Wq, bq, Wk, bk, Wv, bv):
        import jax, jax.numpy as jnp
        import numpy as np
        B, LQ, LK = (8, 256, 256)
        QD, KD, VD = (128, 64, 64)
        q = jnp.einsum('bld,de->ble', query, Wq) + bq
        k = jnp.einsum('bld,de->ble', key, Wk) + bk
        v = jnp.einsum('bld,de->ble', value, Wv) + bv
        scores = jnp.einsum('bqe,bke->bqk', q, k)
        attn = jax.nn.softmax(scores, axis=-1)
        out = jnp.einsum('bqk,bke->bqe', attn, v)
        return out

    def _L1_ffn_ref(x, W_router, b_router, W1, b1, W2, b2):
        import jax, jax.numpy as jnp
        import numpy as np
        N_EMBD = 128
        NUM_EXPERTS = 8
        TOP_K = 2
        D_FF = 4 * N_EMBD
        B, S = (4, 256)
        Bv, Sv, D = x.shape
        flat_x = x.reshape(-1, D)
        T = flat_x.shape[0]
        logits = flat_x @ W_router + b_router
        top_vals, top_idx = jax.lax.top_k(logits, TOP_K)
        neg_inf = jnp.full_like(logits, -jnp.inf)
        sparse_logits = neg_inf.at[jnp.arange(T)[:, None], top_idx].set(top_vals)
        router_weights = jax.nn.softmax(sparse_logits, axis=-1)
        final_output = jnp.zeros_like(flat_x)
        for e in range(NUM_EXPERTS):
            expert_mask = jnp.any(top_idx == e, axis=-1)
            h = jax.nn.relu(flat_x @ W1[e] + b1[e])
            y = h @ W2[e] + b2[e]
            w = router_weights[:, e] * expert_mask.astype(x.dtype)
            final_output = final_output + y * w[:, None]
        return final_output.reshape(Bv, Sv, D)
    x = _layernorm(x + _L0_attn_ref(x, L0_attn_W_attn, L0_attn_b_attn, L0_attn_W_proj, L0_attn_b_proj), axis=-1)
    x = _layernorm(x + _L0_xattn_ref(x, ctx_512, itok_BxS2xS_0_7, L0_xattn_proj_in, L0_xattn_proj_out), axis=-1)
    x = _layernorm(x + _L0_ffn_ref(x, L0_ffn_W_gate, L0_ffn_b_gate, L0_ffn_W1, L0_ffn_b1, L0_ffn_W2, L0_ffn_b2), axis=-1)
    x = _layernorm(x + _L1_attn_ref(x), axis=-1)
    x = _layernorm(x + _L1_xattn_ref(x, ctx_512, ctx_512, L1_xattn_Wq, L1_xattn_bq, L1_xattn_Wk, L1_xattn_bk, L1_xattn_Wv, L1_xattn_bv), axis=-1)
    x = _layernorm(x + _L1_ffn_ref(x, L1_ffn_W_router, L1_ffn_b_router, L1_ffn_W1, L1_ffn_b1, L1_ffn_W2, L1_ffn_b2), axis=-1)
    return x

_drawn_inputs = setup_inputs


def setup_inputs(seed=0):
    import zlib

    import numpy as np

    out = dict(_drawn_inputs(seed))
    spreads = {'L0_attn_b_attn': (0.0, 0.1),
     'L0_attn_b_proj': (0.0, 0.1),
     'L1_xattn_bq': (0.0, 0.8),
     'L1_xattn_bk': (0.0, 0.8),
     'L1_xattn_bv': (0.0, 0.1),
     'L1_ffn_b_router': (0.0, 0.1),
     'L1_ffn_b1': (0.0, 0.1),
     'L1_ffn_b2': (0.0, 0.1)}
    factors = {'L1_xattn_Wq': 5.546, 'L1_xattn_Wk': 4.942}
    for name, (base, spread) in spreads.items():
        noise = np.random.default_rng([zlib.crc32(name.encode()), seed]).standard_normal(out[name].shape)
        drawn = base * np.exp(spread * noise) if base else spread * noise
        out[name] = jnp.asarray(drawn.astype(out[name].dtype))
    for name, factor in factors.items():
        out[name] = (out[name] * factor).astype(out[name].dtype)
    return out
```

```python
from contextlib import ExitStack

import concourse.bass as bass
from concourse import mybir

F32 = mybir.dt.float32
F32R = mybir.dt.float32r
BF16 = mybir.dt.bfloat16
I32 = mybir.dt.int32
U32 = mybir.dt.uint32
ALU = mybir.AluOpType
ACT = mybir.ActivationFunctionType
AX = mybir.AxisListType

P = 128
D = 128
S = 64
TILES = 4
G = TILES * P
SEQS = G // S
STREAMS = 2
H = 16
HD = D // H
PAIRS = H // 2
E = 8
CD = 64
VW = 4 * HD + 2
LIGHT = 4
EPS = 1e-5
LNS = 6
CHUNKS = {2: 2, 3: 1, 6: 4}
ATT_SCALE = float(HD) ** -0.5
CLEARED = 1 + 2 * STREAMS
CONSTS_IN = 32
ACT_SET_UP = 3
ATT_PACK = [("ident", P, P), ("parity", P, 2), ("pair_mask", P, PAIRS), ("vmask", P, D), ("outmask", P, 2),
            ("mean_w", P, P), ("iota", P, E), ("eps", P, 1), ("w_attn", P, 3 * D),
            ("b_attn", P, 3), ("w_proj", P, D), ("b_proj", 1, D), ("w_xk", CD, D), ("b_xk", P, 1), ("w_xv", CD, D)]
FFN_PACK = [("w_xq", P, D), ("b_xq", P, 1), ("b_xv", P, D)] + [
    x for st in (3, 6) for x in ((f"b_in{st}", P, E * CHUNKS[st]), (f"b_out{st}", E, D),
                                 (f"w_gate{st}", P, E), (f"b_gate{st}", P, E))]
MASK_PACK = [("identb", P, P), ("causal", P, PAIRS * S)]


def width(columns):
    return sum(n for _, _, n in columns)


PIECE = 512
PIECES = sum(CHUNKS.values()) * E * P // PIECE

SPLIT_EARLY = (CHUNKS[2] + CHUNKS[3]) * E * P // PIECE


def piece_at(k):
    a = k * PIECE
    for st, n in CHUNKS.items():
        if a < n * E * P:
            return st, a
        a -= n * E * P


SPLIT = (0, 1, 4)
WHOLE = (1, 3, 4)
EXP_LN_SET = "natural_log_exp_and_others"


def norm(s, n):
    turn = [("ln_turn", s, n)] if n in SPLIT + WHOLE else []
    return [("ln_stats", s, n), ("ln_scale", s, n)] + turn + ([("ln_split", s, n)] if n in SPLIT else [])


def attention(s):
    out = [("att_in", s), ("ctx_in", s), ("att_qk", s), ("att_v", s), ("ctx_kv", s)]
    out += [("att_keys", s, 0), ("att_keys", s, 1)]
    for b in range(SEQS + 2):
        if b < SEQS:
            out.append(("att_scores", s, b))
        if b in (2, 4):
            out.append(("att_keys", s, b // 2 + 1))
        if 1 <= b <= SEQS:
            out.append(("att_turn", s, b - 1))
        if b >= 2:
            out.append(("att_values", s, b - 2))
        if b == SEQS // 2 + 2:
            out.append(("att_join", s, 0))
    return out + [("gates", s), ("att_join", s, 1), ("att_out", s)] + norm(s, 0)


def experts(s, stage):
    out = [("up", s, stage, 0)]
    for e in range(E):
        if e + 1 < E:
            out.append(("up", s, stage, e + 1))
        out.append(("down", s, stage, e))
    return out


def router(s, stage):
    return [("router", s, stage), ("gateT", s, stage), ("biases", s, stage)]


def middle(s):
    return ([("cummean", s)] + norm(s, 3) + [("x_q", s), ("x_scores", s), ("x_turn", s), ("x_values", s)]
            + norm(s, 4) + router(s, 6))


def weave(heavy, light):
    out, done = [], 0
    for n, step in enumerate(heavy):
        out.append(step)
        upto = len(light) * (n + 1) // len(heavy)
        out += light[done:upto]
        done = upto
    return out


def plan():
    splits = [("w_split", 0, k) for k in range(PIECES)]
    first = (weave(attention(0), splits[:SPLIT_EARLY]) + experts(0, 2) + norm(0, 1) + router(0, 3) + weave(experts(0, 3), splits[SPLIT_EARLY:])
             + norm(0, 2) + middle(0))
    att0, mid0, mid1 = attention(0), middle(0), middle(1)
    cut = len(att0) // 2
    now = lambda steps: [(x, 0) for x in steps]
    ahead = lambda steps: [(x, 1) for x in steps]
    body = (weave(now(experts(0, 6)), now(attention(1)))
            + weave(now(experts(1, 2)), now(norm(0, 5)) + ahead(att0[:cut]))
            + weave(ahead(att0[cut:]), now(norm(1, 1) + router(1, 3)))
            + now(experts(1, 3))
            + weave(ahead(experts(0, 2)), now(norm(1, 2) + mid1))
            + ahead(norm(0, 1) + router(0, 3)) + ahead(experts(0, 3))
            + weave(now(experts(1, 6)), ahead(norm(0, 2) + mid0))
            + now(norm(1, 5)))
    last = (weave(experts(0, 6), attention(1)) + weave(experts(1, 2), norm(0, 5)) + norm(1, 1) + router(1, 3)
            + experts(1, 3) + norm(1, 2) + middle(1) + experts(1, 6) + norm(1, 5))
    return now(first), body, now(last)


LIGHT_USES = {"att_in": 1, "att_qk": 2, "att_v": 2, "ctx_in": 2, "ctx_kv": 2, "att_scores": 1, "att_turn": 1,
              "att_values": 1, "att_join": 1, "att_out": 1, "ln_turn": 1, "router": 1, "gateT": 1, "biases": 1,
              "cummean": 1, "x_q": 1, "x_scores": 1, "x_turn": 1, "x_values": 2}
LINKS = {"att_scores": 1, "att_values": 2, "ln_stats": 2, "ln_scale": 3, ("router", 3): 5, ("router", 6): 8,
         "x_scores": 1, "x_values": 2}


def counts(step):
    kind = step[0]
    return {"light": LIGHT_USES.get(kind, 0), "link": LINKS.get(kind, LINKS.get((kind, step[-1]), 0)),
            "chunk": CHUNKS[step[2]] if kind == "up" else 0, "expert": kind == "down"}


class Part:

    def __init__(self, steps, before, passes):
        self.steps, self.before, self.each, self.passes = steps, dict(before), {}, passes
        run = {k: 0 for k in before}
        for step, _ in steps:
            self.each[step] = dict(run)
            for k, n in counts(step).items():
                run[k] += n
        self.total = run

    def at(self, it):
        return Place(self, it)


class Place:

    def __init__(self, part, it):
        self.part, self.it = part, it
        self.looped = not isinstance(it, int)

    def first(self, what, step):
        return self.part.each[step][what]

    def count(self, what, n, ring=1):
        whole = (self.part.before[what] + n) // ring
        return self.it * (self.part.total[what] // ring) + whole if self.looped else whole

    def nth(self, ahead, per, more):
        return self.it * per + (ahead * per + more)


def decoder(nc, t):
    passes = t["x"].shape[0] * S // G // STREAMS
    zero = {"light": 0, "link": 0, "chunk": 0, "expert": 0}
    head, body, tail = plan()
    head = Part(head, zero, passes)
    body = Part(body, head.total, passes)
    tail = Part(tail, {k: head.total[k] + (passes - 1) * body.total[k] for k in zero}, passes)
    assert all(x.total[k] % n == 0 for x in (head, body) for k, n in (("light", LIGHT), ("chunk", 2), ("expert", 2)))

    with ExitStack() as ctx:
        def sb(name, shape, dt=F32):
            return ctx.enter_context(nc.sbuf_tensor(name, shape, dt))

        def sem(name):
            return ctx.enter_context(nc.semaphore(name))

        def sems(name, n):
            return [sem(f"{name}{i}") for i in range(n)]

        def cut(tile, columns):
            out, at = {}, 0
            for name, rows, n in columns:
                out[name] = tile[0:rows, at:at + n]
                at += n
            return out

        att_pack = sb("att_pack", [P, width(ATT_PACK)])
        ffn_pack = sb("ffn_pack", [P, width(FFN_PACK)])
        mask_pack = sb("mask_pack", [P, width(MASK_PACK)], BF16)
        small = cut(att_pack, ATT_PACK) | cut(ffn_pack, FFN_PACK) | cut(mask_pack, MASK_PACK)
        ident, parity, pair_mask, vmask, outmask = (small[k] for k in ("ident", "parity", "pair_mask", "vmask", "outmask"))
        mean_w, iota, eps = (small[k] for k in ("mean_w", "iota", "eps"))
        w_attn, b_attn, w_proj, b_proj = (small[k] for k in ("w_attn", "b_attn", "w_proj", "b_proj"))
        w_xq, b_xq, w_xk, b_xk, w_xv, b_xv = (small[k] for k in ("w_xq", "b_xq", "w_xk", "b_xk", "w_xv", "b_xv"))
        identb, causal = small["identb"], small["causal"]
        b_in, b_out, w_gate, b_gate = ({st: small[f"{k}{st}"] for st in (3, 6)}
                                       for k in ("b_in", "b_out", "w_gate", "b_gate"))
        bq_masked = sb("bq_masked", [P, 2])
        att_bias = sb("att_bias", [P, D])
        w_raw = sb("w_raw", [P, 2, PIECE])
        w_hi = {st: sb(f"w_hi{st}", [P, E, CHUNKS[st] * P], F32R) for st in CHUNKS}
        w_lo = {st: sb(f"w_lo{st}", [P, E, CHUNKS[st] * P], F32R) for st in CHUNKS}
        w_out = {st: sb(f"w_out{st}", [P, E, CHUNKS[st], D]) for st in CHUNKS}

        def each(name, shape, dt=F32):
            return [sb(f"{name}{s}", shape, dt) for s in range(STREAMS)]

        xin = each("xin", [P, TILES, D])
        ctx_k = each("ctx_k", [CD, SEQS, S])
        ctx_l = each("ctx_l", [P, TILES, S])
        tok_i = each("tok_i", [CD, SEQS, S], I32)
        x = each("x", [P, TILES, D])
        z = each("z", [P, TILES, D])
        xT = each("xT", [P, G])
        x_hi = each("x_hi", [P, G], F32R)
        x_lo = each("x_lo", [P, G], F32R)
        gate = each("gate", [P, TILES, E])
        gate2 = each("gate2", [P, TILES, E])
        xkT = each("xkT", [P, G])
        xv = each("xv", [P, TILES, D + 2])
        probs2 = each("probs2", [P, TILES, P])
        stats = each("stats", [P, TILES, 6])
        meanvar = each("meanvar", [P, TILES, 2])
        var_eps = each("var_eps", [P, TILES])
        ln_var = each("ln_var", [P, TILES])
        rough = each("rough", [P, TILES])
        newton = each("newton", [P, 2, TILES])
        rstd = each("rstd", [P, TILES])

        q_m = sb("q_m", [P, SEQS, 2, S])
        kT = sb("kT", [P, SEQS, S])
        k_x = sb("k_x", [P, 2, 2, PAIRS, S])
        v_x = sb("v_x", [P, SEQS, TILES, VW])
        row_max = sb("row_max", [P, 2, PAIRS])
        shifted = sb("shifted", [P, 2, PAIRS, S])
        probs = shifted[:].rearrange("p r a k -> p r (a k)")
        probsT = sb("probsT", [P, 2, TILES, P])
        inv_sum = sb("inv_sum", [P, TILES, 2])
        inv_mask = sb("inv_mask", [P, PAIRS, 2])
        heads = sb("heads", [P, SEQS, D])
        x_twice = sb("x_twice", [P, SEQS, 2, S])
        headsT = x_twice[:].rearrange("p b a q -> p (b a q)").rearrange("p (a b q) -> p a b q", a=2, b=SEQS)
        tok_f = [a[:].bitcast(F32) for a in tok_i]
        ctxT = sb("ctxT", [CD, G])
        gate_src = sb("gate_src", [P, 2, TILES * S])
        picked = sb("picked", [P, E, TILES * S])
        hidden = sb("hidden", [P, 2, max(CHUNKS.values()), G])
        logits = sb("logits", [P, TILES, E])
        top = sb("top", [P, TILES, 8])
        top_at = sb("top_at", [P, TILES, 8], U32)
        top_atf = sb("top_atf", [P, TILES, 2])
        top_w = sb("top_w", [P, TILES, 2])
        gap = sb("gap", [P, TILES])
        gap_exp = sb("gap_exp", [P, TILES])
        exp_1 = sb("exp_1", [P, TILES])
        mask_f32 = picked[:].rearrange("p e c -> p (e c)")[:, 0:width(MASK_PACK)]
        idle = sb("idle", [P, 1])
        idle_pool = sb("idle_pool", [P, 1])
        hit = sb("hit", [P, TILES, 2, E])
        gateT = ctxT[0:E].rearrange("p (t q) -> p t q", t=TILES)
        xqT = heads[:, 0:SEQS // 2].rearrange("p b d -> p (b d)")
        max2 = sb("max2", [P, TILES])
        shifted2 = q_m[:, 0:2].rearrange("p b a q -> p (b a) q")
        probs2T = heads[:, SEQS // 2:SEQS]
        inv2 = sb("inv2", [P, TILES])

        light = ctx.enter_context(nc.psum_tensor("light", [P, LIGHT, 512], F32))
        hid = ctx.enter_context(nc.psum_tensor("hid", [P, 2, 512], F32))
        mix = ctx.enter_context(nc.psum_tensor("mix", [P, 2, 512], F32))

        consts_in = sem("consts_in")
        small_in = sem("small_in")
        w_raw_in = sems("w_raw_in", 2)
        w_out_in = {st: sem(f"w_out_in{st}") for st in CHUNKS}
        w_hi_done = sem("w_hi_done")
        w_lo_done = sem("w_lo_done")
        x_stored = sems("x_stored", STREAMS)
        x_hi_done = sems("x_hi_done", STREAMS)
        ln_var_done = sems("ln_var_done", STREAMS)
        is_e_done = sem("is_e_done")
        x_in = sems("x_in", STREAMS)
        ctx_in = sems("ctx_in", STREAMS)
        x_out = sems("x_out", STREAMS)
        light_full = sems("light_full", LIGHT)
        light_done = sems("light_done", LIGHT)
        hid_full = sems("hid_full", 2)
        hid_done = sems("hid_done", 2)
        mix_full = sems("mix_full", 2)
        mix_done = sems("mix_done", 2)
        cleared = sem("cleared")
        ones_set = sem("ones_set")
        act_set_up = sem("act_set_up")
        bias_full = sem("bias_full")
        bias_done = sem("bias_done")
        biased = sems("biased", STREAMS)
        k_x_done = sem("k_x_done")
        scores_read = sem("scores_read")
        exp_done = sems("exp_done", 2)
        tok_done = sem("tok_done")
        picked_done = sem("picked_done")
        gate2_done = sem("gate2_done")
        var_done = sems("var_done", STREAMS)
        rough_done = sems("rough_done", STREAMS)
        x_done = sems("x_done", STREAMS)
        gate_done = sems("gate_done", STREAMS)
        gap_done = sem("gap_done")
        gap_exp_done = sem("gap_exp_done")
        probs2_done = sem("probs2_done")
        dve_step = sem("dve_step")

        x_tiles = t["x"].rearrange("(g t b) q d -> (b q) g t d", g=passes * STREAMS, t=TILES)
        out_tiles = t["out"].rearrange("(g t b) q d -> (b q) g t d", g=passes * STREAMS, t=TILES)
        ctx_tiles = t["ctx_512"].rearrange("(g t b) k c -> (b k) g t c", g=passes * STREAMS, t=TILES)
        ctx_seqs = t["ctx_512"].rearrange("(g b) k c -> k g b c", g=passes * STREAMS)
        tok_seqs = t["tok"].rearrange("(g b) k c -> k g b c", g=passes * STREAMS)

        def piece(parts, k):
            st, a = piece_at(k)
            return parts[st][:].rearrange("p e h -> p (e h)")[:, a:a + PIECE]

        block = ctx.enter_context(nc.Block())

        @block.sync
        def _(sp):
            def load(s, group):
                sp.dma_start(xin[s][:], x_tiles[:, bass.ds(group, 1)].rearrange("p g t d -> p (g t) d")).then_inc(x_in[s], 16)
                sp.dma_start(ctx_l[s][:], ctx_tiles[:, bass.ds(group, 1)].rearrange("p g t c -> p (g t) c")).then_inc(ctx_in[s], 16)
                sp.dma_start(ctx_k[s][:], ctx_seqs[:, bass.ds(group, 1)].rearrange("p g b c -> p (g b) c")).then_inc(ctx_in[s], 16)
                sp.dma_start(tok_i[s][:], tok_seqs[:, bass.ds(group, 1)].rearrange("p g b c -> p (g b) c")).then_inc(ctx_in[s], 16)

            def store(s, group):
                sp.dma_start(out_tiles[:, bass.ds(group, 1)].rearrange("p g t d -> p (g t) d"), x[s][:]).then_inc(x_out[s], 16)

            for s in range(STREAMS):
                sp.sem_inc(x_stored[s], 1)
            for s in range(STREAMS):
                load(s, s)
            for k in range(PIECES):
                if k >= 2:
                    sp.wait_ge(w_lo_done, k - 1)
                st, a = piece_at(k)
                sp.dma_start(w_raw[:, k % 2], t[f"w_in{st}"].rearrange("p e h -> p (e h)")[:, a:a + PIECE]
                             ).then_inc(w_raw_in[k % 2], 16)
            with sp.Fori(0, passes - 1) as it:
                for s in range(STREAMS):
                    sp.wait_ge(x_done[s], it * LNS + 1)
                    sp.wait_ge(x_done[s], 1)
                    load(s, it * STREAMS + (STREAMS + s))
                for s in range(STREAMS):
                    sp.wait_ge(x_done[s], it * LNS + LNS)
                    sp.wait_ge(x_done[s], LNS)
                    store(s, it * STREAMS + s)
                    sp.wait_ge(x_out[s], it * 16 + 16)
                    sp.sem_inc(x_stored[s], 1)
            for s in range(STREAMS):
                sp.wait_ge(x_done[s], passes * LNS)
                store(s, (passes - 1) * STREAMS + s)
            for s in range(STREAMS):
                sp.wait_ge(x_out[s], 16 * passes)

        @block.gpsimd
        def _(pool):
            pool.memset(v_x[:], 0.0).then_inc(cleared, 1)
            for s in range(STREAMS):
                pool.memset(xv[s][:], 1.0).then_inc(cleared, 1)
                pool.memset(probs2[s][:], 0.0).then_inc(cleared, 1)
            pool.wait_ge(cleared, CLEARED)
            for pl in range(2):
                rows = slice(S * pl, S * pl + S)
                pool.memset(v_x[rows, :, :, 4 * HD + pl], 1.0).then_inc(ones_set, 1)
                pool.wait_ge(ones_set, pl + 1)
            pool.wait_ge(consts_in, CONSTS_IN)

            def run(at):
                def read_out(step, more=0):
                    u = at.first("light", step) + more
                    pool.wait_ge(light_done[u % LIGHT], at.count("light", u, LIGHT) + 1)

                def full(step):
                    u = at.first("light", step)
                    pool.wait_ge(light_full[u % LIGHT], at.count("light", u, LIGHT) + 1)

                for step, ahead in at.part.steps:
                    kind, s = step[:2]
                    if kind == "att_in":
                        full(step)
                        pool.wait_ge(bias_done, 1)
                        pool.tensor_tensor(xin[s][:], xin[s][:],
                                           att_bias[:].unsqueeze(1).to_broadcast([P, TILES, D]),
                                           ALU.add).then_inc(biased[s], 1)
                    elif kind == "ctx_in":
                        read_out(step)
                        pool.tensor_tensor(idle_pool[:], eps, eps, ALU.mult)
                        for e in range(E):
                            pool.tensor_scalar(picked[:, e], gate_src[:, 1], float(e), None,
                                               ALU.is_equal).then_inc(is_e_done, 1)
                            pool.wait_ge(is_e_done, at.nth(ahead, E * STREAMS, s * E + e + 1))
                            pool.tensor_tensor(picked[:, e], picked[:, e], gate_src[:, 0],
                                               ALU.mult).then_inc(picked_done, 1)
                    elif kind == "ln_turn" and step[2] == 3:
                        full(step)
                        pool.tensor_tensor(x[s][:], x[s][:], b_xv.unsqueeze(1).to_broadcast([P, TILES, D]),
                                           ALU.add).then_inc(biased[s], 1)

            run(head.at(0))
            with pool.Fori(0, passes - 1) as it:
                run(body.at(it))
            run(tail.at(passes - 1))

        @block.scalar
        def _(act):
            act.preload_act_table_set(EXP_LN_SET)
            act.dma_start(att_pack[:], t["att_pack"]).then_inc(consts_in, 16)
            act.dma_start(mask_f32, t["mask_pack"]).then_inc(consts_in, 16)
            for st in CHUNKS:
                if st == 3:
                    act.dma_start(ffn_pack[:], t["ffn_pack"]).then_inc(small_in, 16)
                act.dma_start(w_out[st][:], t[f"w_out{st}"]).then_inc(w_out_in[st], 16)
            act.wait_ge(consts_in, CONSTS_IN)
            for par in range(2):
                act.activation(bq_masked[:, par:par + 1], b_attn[:, 0:1], ACT.Identity,
                               scale=parity[:, par:par + 1]).then_inc(act_set_up, 1)
            act.activation(mask_pack[:], mask_f32, ACT.Copy).then_inc(act_set_up, 1)
            act.wait_ge(act_set_up, ACT_SET_UP)
            act.wait_ge(cleared, CLEARED)
            act.wait_ge(bias_full, 1)
            act.activation(att_bias[:], hid[:, 1, 0:D], ACT.Copy).then_inc(bias_done, 1)
            act.wait_ge(bias_done, 1)

            def run(at):
                def full(u):
                    act.wait_ge(light_full[u % LIGHT], at.count("light", u, LIGHT) + 1)

                def read_out(u):
                    act.wait_ge(light_done[u % LIGHT], at.count("light", u, LIGHT) + 1)

                def bank(u):
                    return light[:, u % LIGHT]

                for step, ahead in at.part.steps:
                    kind, s = step[:2]
                    u = at.first("light", step)
                    seqs = lambda a: a.rearrange("p (b q) -> p b q", b=SEQS)
                    tiles = lambda a: a.rearrange("p (t q) -> p t q", t=TILES)
                    if kind == "w_split":
                        k = step[2]
                        act.wait_ge(w_raw_in[k % 2], 16 * (k // 2) + 16)
                        act.activation(piece(w_hi, k), w_raw[:, k % 2], ACT.Copy).then_inc(w_hi_done, 1)
                    if kind == "att_in":
                        full(u)
                        act.activation(xT[s][:], bank(u), ACT.Copy)
                        for a in range(2):
                            ins = act.activation(x_twice[:, :, a], seqs(bank(u)), ACT.Copy)
                        ins.then_inc(light_done[u % LIGHT], 1)
                    elif kind == "att_qk":
                        full(u)
                        act.wait_ge(scores_read, at.nth(ahead, STREAMS * SEQS, s * SEQS))
                        for par in range(2):
                            ins = act.activation(q_m[:, :, par], seqs(bank(u)), ACT.Identity,
                                                 bias=bq_masked[:, par:par + 1], scale=parity[:, par:par + 1])
                        ins.then_inc(light_done[u % LIGHT], 1)
                        full(u + 1)
                        act.wait_ge(k_x_done, at.nth(ahead, STREAMS * SEQS // 2, s * SEQS // 2))
                        act.activation(kT[:], seqs(bank(u + 1)), ACT.Identity,
                                       bias=b_attn[:, 1:2]).then_inc(light_done[(u + 1) % LIGHT], 1)
                    elif kind == "ctx_in":
                        full(u + 1)
                        act.activation(ctxT[:], bank(u + 1)[0:CD], ACT.Copy).then_inc(light_done[(u + 1) % LIGHT], 1)
                    elif kind == "ctx_kv":
                        full(u)
                        act.activation(xkT[s][:], bank(u), ACT.Identity,
                                       bias=b_xk[:, 0:1]).then_inc(light_done[u % LIGHT], 1)
                        full(u + 1)
                        act.activation(xv[s][:, :, 0:D], tiles(bank(u + 1)),
                                       ACT.Copy).then_inc(light_done[(u + 1) % LIGHT], 1)
                    elif kind == "att_scores":
                        r = step[2] % 2
                        read_out(u)
                        act.activation(probs[:, r], shifted[:, r].rearrange("p a k -> p (a k)"), ACT.Exp,
                                       scale=ATT_SCALE).then_inc(exp_done[r], 1)
                    elif kind == "att_turn":
                        full(u)
                        act.activation(probsT[:, step[2] % 2], tiles(bank(u)), ACT.Copy).then_inc(light_done[u % LIGHT], 1)
                    elif kind == "att_join":
                        full(u)
                        j = step[2]
                        act.activation(headsT[:, :, 4 * j:4 * j + 4].rearrange("p a b q -> p b a q"),
                                       bank(u).rearrange("p (b a q) -> p b a q", b=4, a=2),
                                       ACT.Copy).then_inc(light_done[u % LIGHT], 1)
                    elif kind == "ln_stats":
                        n = step[2] + 1
                        act.wait_ge(var_done[s], at.nth(ahead, LNS, n))
                        act.activation(ln_var[s][:], meanvar[s][:, :, 1], ACT.Ln, bias=eps[:, 0:1]).then_inc(ln_var_done[s], 1)
                        act.wait_ge(ln_var_done[s], at.nth(ahead, LNS, n))
                        act.activation(rough[s][:], ln_var[s][:], ACT.Exp, scale=-0.5).then_inc(rough_done[s], 1)
                    elif kind == "ln_turn":
                        full(u)
                        if step[2] in WHOLE:
                            ins = act.activation(xT[s][:], bank(u), ACT.Copy)
                        if step[2] in SPLIT:
                            act.activation(x_hi[s][:], bank(u), ACT.Copy).then_inc(x_hi_done[s], 1)
                        else:
                            ins.then_inc(light_done[u % LIGHT], 1)
                    elif kind == "up":
                        stage, e = step[2:]
                        m = at.first("expert", ("down", s, stage, e))
                        for c in range(CHUNKS[stage]):
                            n = at.first("chunk", step) + c
                            act.wait_ge(hid_full[n % 2], at.count("chunk", n, 2) + 1)
                            if c == 0:
                                act.wait_ge(mix_full[m % 2], at.count("expert", m, 2))
                            k = e * CHUNKS[stage] + c
                            act.activation(hidden[:, m % 2, c], hid[:, n % 2], ACT.Relu,
                                           bias=b_in[stage][:, k:k + 1] if stage in b_in else 0.0
                                           ).then_inc(hid_done[n % 2], 1)
                    elif kind == "router" and step[2] == 6:
                        act.wait_ge(gap_done, at.nth(ahead, STREAMS, s + 1))
                        act.activation(gap_exp[:], gap[:], ACT.Exp).then_inc(gap_exp_done, 1)
                    elif kind == "gateT":
                        full(u)
                        act.activation(gateT, tiles(bank(u)[0:E]), ACT.Copy).then_inc(light_done[u % LIGHT], 1)
                    elif kind == "x_q":
                        full(u)
                        act.activation(xqT, bank(u), ACT.Identity, bias=b_xq[:, 0:1]).then_inc(light_done[u % LIGHT], 1)
                    elif kind == "x_scores":
                        read_out(u)
                        for hb in range(2):
                            rows = slice(S * hb, S * hb + S)
                            act.activation(probs2[s][rows, :, S * hb:S * hb + S], shifted2[rows],
                                           ACT.Exp).then_inc(probs2_done, 1)
                    elif kind == "x_turn":
                        full(u)
                        act.activation(probs2T, tiles(bank(u)), ACT.Copy).then_inc(light_done[u % LIGHT], 1)

            act.wait_ge(small_in, 16)
            run(head.at(0))
            with act.Fori(0, passes - 1) as it:
                act.preload_act_table_set(EXP_LN_SET)
                run(body.at(it))
            run(tail.at(passes - 1))

        @block.vector
        def _(dve):
            dve.wait_ge(consts_in, CONSTS_IN)
            dve.wait_ge(cleared, CLEARED)
            dve.wait_ge(ones_set, 2)
            dve.wait_ge(small_in, 16)

            def run(at):
                linked = [0, 0]

                def link(ins):
                    ins.then_inc(dve_step, 1)
                    dve.wait_ge(dve_step, at.count("link", linked[0]) + 1)
                    linked[0] += 1

                def full(u):
                    dve.wait_ge(light_full[u % LIGHT], at.count("light", u, LIGHT) + 1)
                    return light[:, u % LIGHT]

                def link_bank(u, ins):
                    ins.then_inc(light_done[u % LIGHT], 1)
                    dve.wait_ge(light_done[u % LIGHT], at.count("light", u, LIGHT) + 1)

                def carry_wait():
                    dve.memset(idle[:], 0.0)

                tiles = lambda a: a.rearrange("p (t c) -> p t c", t=TILES)
                flat = lambda a: a.rearrange("p t d -> p (t d)")
                for step, ahead in at.part.steps:
                    kind, s = step[:2]
                    u = at.first("light", step)
                    assert linked[0] == at.first("link", step), step
                    if kind == "w_split":
                        k = step[2]
                        dve.wait_ge(w_hi_done, k + 1)
                        dve.tensor_tensor(piece(w_lo, k), w_raw[:, k % 2], piece(w_hi, k).bitcast(F32),
                                          ALU.subtract).then_inc(w_lo_done, 1)
                    elif kind == "att_keys":
                        n = step[2]
                        if n == 0:
                            u = at.first("light", ("att_qk", s)) + 1
                            dve.wait_ge(light_done[u % LIGHT], at.count("light", u, LIGHT) + 1)
                        dve.wait_ge(scores_read, at.nth(ahead, STREAMS * SEQS, s * SEQS + max(0, 2 * n - 2)))
                        for j in range(PAIRS):
                            ins = dve.tensor_scalar(k_x[:, n % 2, :, j, :], kT[:, 2 * n:2 * n + 2], pair_mask[:, j:j + 1],
                                                    None, ALU.mult)
                        ins.then_inc(k_x_done, 1)
                    elif kind == "att_v":
                        for half in range(2):
                            v = full(u + half)
                            for i in range(4):
                                ins = dve.tensor_tensor(v_x[:, 4 * half + i, :, 0:4 * HD],
                                                        tiles(v[:, i * D:(i + 1) * D]), tiles(vmask), ALU.mult)
                            ins.then_inc(light_done[(u + half) % LIGHT], 1)
                    elif kind == "ctx_in":
                        dve.wait_ge(ctx_in[s], at.nth(ahead, 48, 48))
                        dve.tensor_copy(tok_f[s], tok_i[s][:]).then_inc(tok_done, 1)
                        dve.tensor_copy(gate_src[:].rearrange("p a c -> p (a c)"),
                                        full(u)).then_inc(light_done[u % LIGHT], 1)
                    elif kind == "gates":
                        dve.wait_ge(picked_done, at.nth(ahead, E * STREAMS, (s + 1) * E))
                        dve.tensor_reduce(gate2[s][:].rearrange("p t e -> p e t"),
                                          picked[:].rearrange("p e (t k) -> p e t k", t=TILES), AX.X,
                                          ALU.add).then_inc(gate2_done, 1)
                        dve.wait_ge(gate2_done, at.nth(ahead, STREAMS, s + 1))
                    elif kind == "att_scores":
                        r = step[2] % 2
                        n = (s * SEQS + step[2]) // 2
                        sc = full(u).rearrange("p (a k) -> p a k", a=PAIRS)
                        link(dve.tensor_reduce(row_max[:, r], sc, AX.X, ALU.max))
                        dve.wait_ge(exp_done[r], at.nth(ahead, SEQS * STREAMS // 2, n))
                        dve.tensor_tensor(shifted[:, r], sc,
                                          row_max[:, r].unsqueeze(2).to_broadcast([P, PAIRS, S]),
                                          ALU.subtract).then_inc(light_done[u % LIGHT], 1)
                    elif kind == "att_values":
                        o = tiles(full(u)[:, 0:TILES * VW])
                        link(dve.reciprocal(inv_sum[:], o[:, :, 4 * HD:4 * HD + 2]))
                        link(dve.tensor_tensor(inv_mask[:],
                                               inv_sum[:].rearrange("p t a -> p (t a)").unsqueeze(2).to_broadcast([P, PAIRS, 2]),
                                               outmask.unsqueeze(1).to_broadcast([P, PAIRS, 2]), ALU.mult))
                        dve.tensor_tensor(heads[:, step[2]].rearrange("p (t c d) -> p t c d", t=TILES, d=HD),
                                          o[:, :, 0:4 * HD].rearrange("p t (c d) -> p t c d", d=HD),
                                          inv_mask[:].rearrange("p (t a) b -> p t (a b)", t=TILES).unsqueeze(3)
                                          .to_broadcast([P, TILES, 4, HD]),
                                          ALU.mult).then_inc(light_done[u % LIGHT], 1)
                    elif kind == "att_out":
                        dve.wait_ge(biased[s], at.nth(ahead, 2, 1))
                        y = full(u)
                        link_bank(u, dve.tensor_tensor(flat(z[s][:]), y, flat(xin[s][:]), ALU.add))
                    elif kind == "cummean":
                        y = full(u)
                        link_bank(u, dve.tensor_tensor(flat(z[s][:]), y, flat(x[s][:]), ALU.add))
                    elif kind == "ln_stats":
                        for i in range(TILES):
                            ins = dve.bn_stats(stats[s][:, i], z[s][:, i])
                        link(ins)
                        carry_wait()
                        for i in range(TILES):
                            ins = dve.bn_aggr(meanvar[s][:, i], stats[s][:, i])
                        ins.then_inc(var_done[s], 1)
                        dve.wait_ge(var_done[s], at.nth(ahead, LNS, step[2] + 1))
                        link(dve.tensor_scalar(var_eps[s][:], meanvar[s][:, :, 1], EPS, None, ALU.add))
                    elif kind == "ln_scale":
                        dve.wait_ge(rough_done[s], at.nth(ahead, LNS, step[2] + 1))
                        link(dve.scalar_tensor_tensor(out=newton[s][:, 0], in0=rough[s][:], scalar=-0.5, in1=rough[s][:],
                                                      op0=ALU.mult, op1=ALU.mult))
                        link(dve.tensor_tensor(newton[s][:, 1], newton[s][:, 0], var_eps[s][:], ALU.mult))
                        link(dve.scalar_tensor_tensor(out=rstd[s][:], in0=newton[s][:, 1], scalar=1.5, in1=rough[s][:],
                                                      op0=ALU.add, op1=ALU.mult))
                        if step[2] == 0:
                            dve.wait_ge(x_stored[s], at.nth(ahead, 1, 1))
                        for i in range(TILES):
                            ins = dve.tensor_scalar(x[s][:, i], z[s][:, i], meanvar[s][:, i, 0:1], rstd[s][:, i:i + 1],
                                                    ALU.subtract, ALU.mult)
                        ins.then_inc(x_done[s], 1)
                        dve.wait_ge(x_done[s], at.nth(ahead, LNS, step[2] + 1))
                    elif kind == "ln_split":
                        u = at.first("light", ("ln_turn", s, step[2]))
                        dve.wait_ge(x_hi_done[s], at.nth(ahead, len(SPLIT), SPLIT.index(step[2]) + 1))
                        dve.tensor_tensor(x_lo[s][:], full(u), x_hi[s][:].bitcast(F32),
                                          ALU.subtract).then_inc(light_done[u % LIGHT], 1)
                    elif kind == "down":
                        stage, e = step[2:]
                        m = at.first("expert", step)
                        dve.wait_ge(mix_full[m % 2], at.count("expert", m, 2) + 1)
                        if e > 0:
                            dve.wait_ge(mix_done[(m - 1) % 2], at.count("expert", m - 1, 2) + 1)
                        g = gate2[s] if stage == 2 else gate[s]
                        so_far = x[s] if stage == 2 and e == 0 else z[s]
                        for i in range(TILES):
                            ins = dve.scalar_tensor_tensor(out=z[s][:, i], in0=mix[:, m % 2, i * D:(i + 1) * D],
                                                           scalar=g[:, i, e:e + 1], in1=so_far[:, i],
                                                           op0=ALU.mult, op1=ALU.add)
                        ins.then_inc(mix_done[m % 2], 1)
                        if e == E - 1:
                            dve.wait_ge(mix_done[m % 2], at.count("expert", m, 2) + 1)
                    elif kind == "router":
                        stage = step[2]
                        link_bank(u, dve.tensor_tensor(logits[:], tiles(full(u)[:, 0:TILES * E]),
                                                       b_gate[stage].unsqueeze(1).to_broadcast([P, TILES, E]), ALU.add))
                        carry_wait()
                        for i in range(TILES):
                            ins = dve.max(top[:, i], logits[:, i])
                        link(ins)
                        carry_wait()
                        for i in range(TILES):
                            ins = dve.max_index(top_at[:, i], top[:, i], logits[:, i])
                        link(ins)
                        link(dve.tensor_copy(top_atf[:], top_at[:, :, 0:2]))
                        weights = top[:, :, 0:2]
                        if stage == 6:
                            dve.tensor_tensor(gap[:], top[:, :, 1], top[:, :, 0], ALU.subtract).then_inc(gap_done, 1)
                            dve.wait_ge(gap_exp_done, at.nth(ahead, STREAMS, s + 1))
                            link(dve.tensor_scalar(exp_1[:], gap_exp[:], 1.0, None, ALU.add))
                            link(dve.reciprocal(top_w[:, :, 0], exp_1[:]))
                            link(dve.tensor_tensor(top_w[:, :, 1], gap_exp[:], top_w[:, :, 0], ALU.mult))
                            weights = top_w[:]
                        link(dve.tensor_tensor(hit[:], iota.unsqueeze(1).unsqueeze(1).to_broadcast([P, TILES, 2, E]),
                                               top_atf[:].unsqueeze(3).to_broadcast([P, TILES, 2, E]), ALU.is_equal))
                        link(dve.tensor_tensor(hit[:], hit[:], weights.unsqueeze(3).to_broadcast([P, TILES, 2, E]),
                                               ALU.mult))
                        dve.tensor_tensor(gate[s][:], hit[:, :, 0], hit[:, :, 1], ALU.add).then_inc(gate_done[s], 1)
                    elif kind == "biases":
                        y = full(u)
                        link_bank(u, dve.tensor_tensor(flat(z[s][:]), y, flat(x[s][:]), ALU.add))
                    elif kind == "x_scores":
                        sc = tiles(full(u)[:, 0:TILES * S])
                        link(dve.tensor_reduce(max2[:], sc, AX.X, ALU.max))
                        dve.tensor_tensor(shifted2, sc, max2[:].unsqueeze(2).to_broadcast([P, TILES, S]),
                                          ALU.subtract).then_inc(light_done[u % LIGHT], 1)
                    elif kind == "x_values":
                        dve.wait_ge(biased[s], at.nth(ahead, 2, 2))
                        for half in range(2):
                            o = full(u + half)[:, 0:2 * (D + 2)].rearrange("p (t c) -> p t c", t=2)
                            link(dve.reciprocal(inv2[:, 2 * half:2 * half + 2], o[:, :, D]))
                            for i in range(2):
                                n = 2 * half + i
                                ins = dve.scalar_tensor_tensor(out=z[s][:, n], in0=o[:, i, 0:D], scalar=inv2[:, n:n + 1],
                                                               in1=x[s][:, n], op0=ALU.mult, op1=ALU.add)
                            link_bank(u + half, ins)
                assert linked[0] == at.part.total["link"]

            run(head.at(0))
            with dve.Fori(0, passes - 1) as it:
                run(body.at(it))
            run(tail.at(passes - 1))

        @block.tensor
        def _(pe):
            pe.wait_ge(consts_in, CONSTS_IN)
            pe.matmul(hid[:, 1, 0:D], b_attn[:, 2:3].to_broadcast([P, P]), w_proj, start=True, stop=False)
            pe.matmul(hid[:, 1, 0:D], outmask[0:1, 0:1].to_broadcast([1, P]), b_proj, start=False, stop=True).then_inc(bias_full, 1)
            pe.wait_ge(bias_done, 1)
            pe.wait_ge(cleared, CLEARED)
            pe.wait_ge(ones_set, 2)
            pe.wait_ge(act_set_up, ACT_SET_UP)

            def run(at):
                taken = [-1]

                def take(u):
                    pe.wait_ge(light_done[u % LIGHT], at.count("light", u, LIGHT))
                    taken[0] = u
                    return light[:, u % LIGHT]

                def read_out(step, more=0):
                    u = at.first("light", step) + more
                    if u + LIGHT > taken[0]:
                        pe.wait_ge(light_done[u % LIGHT], at.count("light", u, LIGHT) + 1)

                for step, ahead in at.part.steps:
                    kind, s = step[:2]
                    u = at.first("light", step)
                    b = step[2] if len(step) > 2 else None
                    if kind == "att_in":
                        bank = take(u)
                        pe.wait_ge(x_in[s], at.nth(ahead, 16, 16))
                        for i in range(TILES):
                            ins = pe.transpose(bank[:, i * P:(i + 1) * P], xin[s][:, i], ident)
                        ins.then_inc(light_full[u % LIGHT], 1)
                    elif kind == "att_qk":
                        for j in range(2):
                            bank = take(u + j)
                            read_out(("att_in", s))
                            pe.matmul(bank, w_attn[:, j * D:(j + 1) * D], xT[s][:], start=True,
                                      stop=True).then_inc(light_full[(u + j) % LIGHT], 1)
                    elif kind == "att_v":
                        for half in range(2):
                            bank = take(u + half)
                            for i in range(4):
                                ins = pe.matmul(bank[:, i * D:(i + 1) * D],
                                                x_twice[:, 4 * half + i].rearrange("p a q -> p (a q)"),
                                                w_attn[:, 2 * D:3 * D], start=True, stop=True)
                            ins.then_inc(light_full[(u + half) % LIGHT], 1)
                    elif kind == "ctx_in":
                        bank = take(u)
                        pe.wait_ge(ctx_in[s], at.nth(ahead, 48, 48))
                        pe.wait_ge(tok_done, at.nth(ahead, STREAMS, s + 1))
                        take(u + 1)
                        pe.matmul(bank[:, 0:2], identb, identb[:, 0:2], start=True, stop=True)
                        for j, src in enumerate((ctx_k[s], tok_f[s])):
                            for i in range(TILES):
                                ins = pe.transpose(bank[:, j * TILES * S + i * S:j * TILES * S + (i + 1) * S],
                                                   src[:, 2 * i:2 * i + 2].rearrange("p b c -> p (b c)"),
                                                   ident[0:CD, 0:CD])
                        ins.then_inc(light_full[u % LIGHT], 1)
                        bank = light[:, (u + 1) % LIGHT]
                        for i in range(TILES):
                            ins = pe.transpose(bank[0:CD, i * P:(i + 1) * P], ctx_l[s][:, i], ident)
                        ins.then_inc(light_full[(u + 1) % LIGHT], 1)
                    elif kind == "ctx_kv":
                        bank = take(u)
                        read_out(("ctx_in", s), 1)
                        pe.matmul(bank, w_xk, ctxT[:], start=True, stop=True).then_inc(light_full[u % LIGHT], 1)
                        bank = take(u + 1)
                        for i in range(TILES):
                            ins = pe.matmul(bank[:, i * D:(i + 1) * D], ctxT[:, i * P:(i + 1) * P], w_xv,
                                            start=True, stop=True)
                        ins.then_inc(light_full[(u + 1) % LIGHT], 1)
                    elif kind == "att_scores":
                        bank = take(u)
                        if b == 0:
                            read_out(("att_qk", s))
                        if b % 2 == 0:
                            pe.wait_ge(k_x_done, at.nth(ahead, STREAMS * SEQS // 2, s * SEQS // 2 + b // 2 + 1))
                        pe.matmul(bank, q_m[:, b].rearrange("p a q -> p (a q)"), k_x[:, b // 2 % 2, b % 2].rearrange("p a k -> p (a k)"),
                                  start=True, stop=False).then_inc(scores_read, 1)
                        pe.matmul(bank, identb, causal, start=False, stop=True).then_inc(light_full[u % LIGHT], 1)
                    elif kind == "att_turn":
                        bank = take(u)
                        pe.wait_ge(exp_done[b % 2], at.nth(ahead, SEQS * STREAMS // 2, (s * SEQS + b) // 2 + 1))
                        for i in range(TILES):
                            ins = pe.transpose(bank[:, i * P:(i + 1) * P], probs[:, b % 2, i * P:(i + 1) * P], ident)
                        ins.then_inc(light_full[u % LIGHT], 1)
                    elif kind == "att_values":
                        bank = take(u)
                        if b == 0:
                            for half in range(2):
                                read_out(("att_v", s), half)
                        read_out(("att_turn", s, b))
                        for i in range(TILES):
                            ins = pe.matmul(bank[:, i * VW:(i + 1) * VW], probsT[:, b % 2, i], v_x[:, b, i],
                                            start=True, stop=True)
                        ins.then_inc(light_full[u % LIGHT], 1)
                    elif kind == "att_join":
                        bank = take(u)
                        read_out(("att_values", s, 4 * b + 3))
                        for i in range(4):
                            ins = pe.transpose(bank[:, i * P:(i + 1) * P], heads[:, 4 * b + i], ident)
                        ins.then_inc(light_full[u % LIGHT], 1)
                    elif kind == "att_out":
                        bank = take(u)
                        for i in range(TILES):
                            if i % 2 == 0:
                                read_out(("att_join", s, i // 2))
                            for par in range(2):
                                ins = pe.matmul(bank[:, i * D:(i + 1) * D],
                                                headsT[:, par, 2 * i:2 * i + 2].rearrange("p b q -> p (b q)"), w_proj,
                                                start=(par == 0), stop=(par == 1))
                        ins.then_inc(light_full[u % LIGHT], 1)
                    elif kind == "ln_turn":
                        bank = take(u)
                        pe.wait_ge(x_done[s], at.nth(ahead, LNS, b + 1))
                        for i in range(TILES):
                            ins = pe.transpose(bank[:, i * P:(i + 1) * P], x[s][:, i], ident)
                        ins.then_inc(light_full[u % LIGHT], 1)
                    elif kind == "up":
                        stage, e = step[2:]
                        if e == 0:
                            pe.wait_ge(w_lo_done, {2: SPLIT_EARLY - 2, 3: SPLIT_EARLY, 6: PIECES}[stage])
                            if stage == 2:
                                read_out(("ln_turn", s, 0))
                        for c in range(CHUNKS[stage]):
                            n = at.first("chunk", step) + c
                            cols = slice(c * P, (c + 1) * P)
                            pe.wait_ge(hid_done[n % 2], at.count("chunk", n, 2))
                            pe.matmul(hid[:, n % 2], w_hi[stage][:, e, cols], x_lo[s][:], start=True, stop=False)
                            pe.matmul(hid[:, n % 2], w_hi[stage][:, e, cols], x_hi[s][:], start=False, stop=False)
                            pe.matmul(hid[:, n % 2], w_lo[stage][:, e, cols], x_hi[s][:], start=False,
                                      stop=True).then_inc(hid_full[n % 2], 1)
                    elif kind == "down":
                        stage, e = step[2:]
                        m = at.first("expert", step)
                        pe.wait_ge(mix_done[m % 2], at.count("expert", m, 2))
                        if e == 0:
                            pe.wait_ge(w_out_in[stage], 16)
                        cs = CHUNKS[stage]
                        end = at.first("chunk", ("up", s, stage, e)) + cs
                        for n in range(end - min(cs, 2), end):
                            pe.wait_ge(hid_done[n % 2], at.count("chunk", n, 2) + 1)
                        for i in range(TILES):
                            for c in range(cs):
                                ins = pe.matmul(mix[:, m % 2, i * D:(i + 1) * D],
                                                hidden[:, m % 2, c, i * P:(i + 1) * P],
                                                w_out[stage][:, e, c], start=(c == 0), stop=(c == cs - 1))
                        ins.then_inc(mix_full[m % 2], 1)
                    elif kind == "router":
                        bank = take(u)
                        read_out(("ln_turn", s, {3: 1, 6: 4}[b]))
                        pe.wait_ge(small_in, 16)
                        for i in range(TILES):
                            ins = pe.matmul(bank[:, i * E:(i + 1) * E], xT[s][:, i * P:(i + 1) * P], w_gate[b],
                                            start=True, stop=True)
                        ins.then_inc(light_full[u % LIGHT], 1)
                    elif kind == "gateT":
                        bank = take(u)
                        pe.wait_ge(gate_done[s], at.nth(ahead, 2, {3: 1, 6: 2}[b]))
                        for i in range(TILES):
                            ins = pe.transpose(bank[0:E, i * P:(i + 1) * P], gate[s][:, i], ident)
                        ins.then_inc(light_full[u % LIGHT], 1)
                    elif kind == "biases":
                        bank = take(u)
                        read_out(("gateT", s, b))
                        for i in range(TILES):
                            ins = pe.matmul(bank[:, i * D:(i + 1) * D], gateT[:, i], b_out[b], start=True, stop=True)
                        ins.then_inc(light_full[u % LIGHT], 1)
                    elif kind == "cummean":
                        bank = take(u)
                        pe.wait_ge(x_done[s], at.nth(ahead, LNS, 3))
                        pe.matmul(bank, mean_w, x[s][:].rearrange("p t d -> p (t d)"), start=True,
                                  stop=True).then_inc(light_full[u % LIGHT], 1)
                    elif kind == "x_q":
                        bank = take(u)
                        read_out(("ln_turn", s, 3))
                        pe.matmul(bank, w_xq, xT[s][:], start=True, stop=True).then_inc(light_full[u % LIGHT], 1)
                    elif kind == "x_scores":
                        bank = take(u)
                        read_out(("x_q", s))
                        read_out(("ctx_kv", s))
                        for i in range(TILES):
                            for hb in range(2):
                                cols = slice(i * P + hb * S, i * P + hb * S + S)
                                ins = pe.matmul(bank[hb * S:hb * S + S, i * S:(i + 1) * S], xqT[:, cols],
                                                xkT[s][:, cols], start=True, stop=True)
                        ins.then_inc(light_full[u % LIGHT], 1)
                    elif kind == "x_turn":
                        bank = take(u)
                        pe.wait_ge(probs2_done, at.nth(ahead, 2 * STREAMS, 2 * (s + 1)))
                        for i in range(TILES):
                            ins = pe.transpose(bank[:, i * P:(i + 1) * P], probs2[s][:, i], ident)
                        ins.then_inc(light_full[u % LIGHT], 1)
                    elif kind == "x_values":
                        for half in range(2):
                            bank = take(u + half)
                            if half == 0:
                                read_out(("x_turn", s))
                                read_out(("ctx_kv", s), 1)
                            for i in range(2):
                                n = 2 * half + i
                                ins = pe.matmul(bank[:, i * (D + 2):(i + 1) * (D + 2)], probs2T[:, n], xv[s][:, n],
                                                start=True, stop=True)
                            ins.then_inc(light_full[(u + half) % LIGHT], 1)

            run(head.at(0))
            with pe.Fori(0, passes - 1) as it:
                run(body.at(it))
            run(tail.at(passes - 1))


def constants():
    import numpy as np

    p = np.arange(P)
    head = p // HD
    k = np.arange(S)
    causal = np.where(k[None, :] > (p % S)[:, None], -1e30, 0.0)
    row, col = p[:, None], p[None, :]
    same_seq = (row // S) == (col // S)
    f = lambda a: np.ascontiguousarray(a, np.float32)
    return {
        "ident": f(np.eye(P)), "identb": f(np.eye(P)), "causal": f(np.tile(causal, (1, PAIRS))),
        "parity": f((head % 2)[:, None] == np.arange(2)), "pair_mask": f((head // 2)[:, None] == np.arange(PAIRS)),
        "vmask": f((head // 2 % 2)[None, :] == (p // S)[:, None]), "outmask": f((p // S)[:, None] == np.arange(2)),
        "mean_w": f(np.where(same_seq & (row <= col), 1.0 / (col % S + 1), 0.0)),
        "iota": f(np.tile(np.arange(E), (P, 1))), "eps": f(np.full((P, 1), EPS)),
    }


def layouts(i):
    import numpy as np

    c = np.ascontiguousarray

    def second(w):
        return c(w.reshape(E, -1, P, D).transpose(2, 0, 1, 3))

    return {
        "x": i["x"], "ctx_512": i["ctx_512"], "tok": i["itok_BxS2xS_0_7"],
        "w_attn": i["L0_attn_W_attn"], "b_attn": c(i["L0_attn_b_attn"].reshape(3, D).T),
        "w_proj": i["L0_attn_W_proj"], "b_proj": i["L0_attn_b_proj"].reshape(1, D),
        "w_in2": c(i["L0_xattn_proj_in"].transpose(2, 0, 1)), "w_out2": second(i["L0_xattn_proj_out"].transpose(0, 2, 1)),
        "w_in3": c(i["L0_ffn_W1"].transpose(1, 0, 2)), "w_out3": second(i["L0_ffn_W2"]),
        "b_in3": c(i["L0_ffn_b1"].T), "b_out3": i["L0_ffn_b2"],
        "w_gate3": i["L0_ffn_W_gate"], "b_gate3": c(np.tile(i["L0_ffn_b_gate"], (P, 1))),
        "w_xq": i["L1_xattn_Wq"], "b_xq": i["L1_xattn_bq"].reshape(D, 1), "w_xk": i["L1_xattn_Wk"],
        "b_xk": i["L1_xattn_bk"].reshape(D, 1), "w_xv": i["L1_xattn_Wv"], "b_xv": c(np.tile(i["L1_xattn_bv"], (P, 1))),
        "w_in6": c(i["L1_ffn_W1"].transpose(1, 0, 2)), "w_out6": second(i["L1_ffn_W2"]),
        "b_in6": c(i["L1_ffn_b1"].reshape(E, CHUNKS[6], P).transpose(2, 0, 1).reshape(P, -1)), "b_out6": i["L1_ffn_b2"],
        "w_gate6": i["L1_ffn_W_router"], "b_gate6": c(np.tile(i["L1_ffn_b_router"], (P, 1))),
    }


def pack(columns):
    import numpy as np

    out = np.zeros((P, sum(n for _, n in columns)), columns[0][0].dtype)
    at = 0
    for a, n in columns:
        out[:a.shape[0], at:at + n] = a
        at += n
    return out


def kernel(**inputs):
    import numpy as np
    import concourse.bacc as bacc
    from concourse import mybir as _mybir
    from concourse.bass_utils import run_bass_kernel_spmd

    nc = bacc.Bacc("TRN2", target_bir_lowering=False, num_devices=1)
    parts = layouts({k: np.asarray(v) for k, v in inputs.items()}) | constants()
    packs = {"att_pack": ATT_PACK, "ffn_pack": FFN_PACK, "mask_pack": MASK_PACK}
    packed = {k: pack([(parts.pop(name), n) for name, _, n in columns]) for k, columns in packs.items()}
    arrays = {k: np.ascontiguousarray(v) for k, v in (parts | packed).items()}
    handles = {k: nc.dram_tensor(f"in_{k}", a.shape, _mybir.dt.from_np(a.dtype), kind="ExternalInput").ap()
               for k, a in arrays.items()}
    handles["out"] = nc.dram_tensor("out_dram", arrays["x"].shape, _mybir.dt.float32, kind="ExternalOutput").ap()
    decoder(nc, handles)
    r = run_bass_kernel_spmd(nc, [{f"in_{k}": a for k, a in arrays.items()}], core_ids=[0])
    return r.results[0]["out_dram"]
```

```python
from contextlib import ExitStack

import concourse.bass as bass
from concourse import mybir

F32 = mybir.dt.float32
F32R = mybir.dt.float32r
BF16 = mybir.dt.bfloat16
I32 = mybir.dt.int32
U32 = mybir.dt.uint32
ALU = mybir.AluOpType
ACT = mybir.ActivationFunctionType
AX = mybir.AxisListType

P = 128
D = 128
S = 64
TILES = 4
G = TILES * P
SEQS = G // S
STREAMS = 2
H = 16
HD = D // H
PAIRS = H // 2
E = 8
CD = 64
VW = 4 * HD + 2
LIGHT = 4
EPS = 1e-5
LNS = 6
CHUNKS = {2: 2, 3: 1, 6: 4}
ATT_SCALE = float(HD) ** -0.5
CLEARED = 1 + 2 * STREAMS
ATT_PACK = [("ident", P, P), ("parity", P, 2), ("pair_mask", P, PAIRS), ("vmask", P, D), ("outmask", P, 2),
            ("mean_w", P, P), ("iota", P, E), ("eps", P, 1), ("w_attn", P, 3 * D),
            ("b_attn", P, 3), ("w_proj", P, D), ("b_proj", 1, D), ("w_xk", CD, D), ("b_xk", P, 1), ("w_xv", CD, D)]
FFN_PACK = [("w_xq", P, D), ("b_xq", P, 1), ("b_xv", P, D)] + [
    x for st in (3, 6) for x in ((f"b_in{st}", P, E * CHUNKS[st]), (f"b_out{st}", E, D),
                                 (f"w_gate{st}", P, E), (f"b_gate{st}", P, E))]
MASK_PACK = [("identb", P, P), ("causal", P, PAIRS * S)]


def width(columns):
    return sum(n for _, _, n in columns)


PIECE = 512
PIECES = sum(CHUNKS.values()) * E * P // PIECE
RAW = 2 * max(CHUNKS.values())


def piece_at(k):
    a = k * PIECE
    for st, n in CHUNKS.items():
        if a < n * E * P:
            return st, a
        a -= n * E * P


SPLIT = (0, 1, 4)
WHOLE = (1, 3, 4)
GATES_AT = 3
BIASES_AT = 4
EXP_LN_SET = "natural_log_exp_and_others"


def norm(s, n):
    turn = [("ln_turn", s, n)] if n in SPLIT + WHOLE else []
    return [("ln_stats", s, n), ("ln_scale", s, n)] + turn + ([("ln_split", s, n)] if n in SPLIT else [])


def attention(s):
    out = [("att_in", s), ("att_qk", s), ("ctx_in", s), ("att_v", s), ("att_keys", s, 0), ("att_keys", s, 1)]
    for b in range(SEQS + 2):
        if b < SEQS:
            out.append(("att_scores", s, b))
        if b == 1:
            out.append(("ctx_kv", s))
        if b in (2, 4):
            out.append(("att_keys", s, b // 2 + 1))
        if 1 <= b <= SEQS:
            out.append(("att_turn", s, b - 1))
        if b >= 2:
            out.append(("att_values", s, b - 2))
        if b == SEQS // 2 + 2:
            out.append(("att_join", s, 0))
    return out + [("att_join", s, 1), ("att_out", s)] + norm(s, 0) + [("gates", s)]


def products(s, stage):
    out = [("up", s, stage, 0)]
    for e in range(E):
        if e + 1 < E:
            out.append(("up", s, stage, e + 1))
        out.append(("down", s, stage, e))
        if stage != 2 and e == GATES_AT:
            out.append(("gateT", s, stage))
        if stage != 2 and e == BIASES_AT:
            out.append(("biases", s, stage))
    return out


def middle(s):
    return ([("cummean", s)] + norm(s, 3) + [("x_q", s), ("x_scores", s), ("x_turn", s), ("x_values", s)]
            + norm(s, 4) + [("router", s, 6)])


def weave(steps, more):
    out, done = [], 0
    for n, step in enumerate(steps):
        out.append(step)
        upto = len(more) * (n + 1) // len(steps)
        out += more[done:upto]
        done = upto
    return out


SPLITS_AFTER = 8
TURNS = [1, 1, 3, 4, 2, 1, 1, 1, 1, 6, 2, 3, 2, 2, 1, 3, 1, 3, 1, 1, 2, 5, 1, 3, 2, 1, 3, 1, 3, 1, 1, 1,
         3, 1, 6, 1, 1, 3, 2, 1, 1, 2, 1, 2, 1, 4, 2, 5, 1, 1, 1, 1, 1, 1, 1, 2, 1, 7, 1, 2, 1, 5, 1, 2,
         1, 1, 1, 1, 1, 1, 1, 2, 2, 3, 2, 1, 1, 1, 1, 1, 2, 1, 1, 2, 2, 1, 1, 2, 2, 1, 1, 1, 1, 1, 3, 1,
         5, 1, 6, 2, 7, 1, 1, 1, 5, 1, 1, 1, 2, 1, 3, 1, 1, 2, 2, 1, 1, 1, 2, 1, 1, 1, 2, 1, 1, 1]



def interleave(a, b, turns):
    out, lists = [], (list(a), list(b))
    for n, more in enumerate(turns):
        out += lists[n % 2][:more]
        del lists[n % 2][:more]
    assert not lists[0] and not lists[1]
    return out


def plan():
    rest = lambda s: (products(s, 2) + norm(s, 1) + [("router", s, 3)] + products(s, 3) + norm(s, 2) + middle(s)
                      + products(s, 6) + norm(s, 5))
    splits = [("w_split", 0, k) for k in range(PIECES)]
    att = attention(0)
    head = [(x, 0) for x in att[:2] + [("set_up", 0)] + att[2:SPLITS_AFTER] + weave(att[SPLITS_AFTER:], splits)]
    body = interleave([(x, 0) for x in rest(0)] + [(x, 1) for x in attention(0)],
                      [(x, 0) for x in attention(1) + rest(1)], TURNS)
    tail = [(x, ahead) for x, ahead in body if not ahead]
    return head, body, tail


LIGHT_USES = {"att_in": 1, "att_qk": 2, "att_v": 2, "ctx_in": 2, "ctx_kv": 2, "att_scores": 1, "att_turn": 1,
              "att_values": 1, "att_join": 1, "att_out": 1, "ln_turn": 1, "router": 1, "gateT": 1, "biases": 1,
              "cummean": 1, "x_q": 1, "x_scores": 1, "x_turn": 1, "x_values": 2}
LINKS = {"att_scores": 1, "att_values": 2, "ln_stats": 2, "ln_scale": 3, ("router", 3): 5, ("router", 6): 8,
         "x_scores": 1, "x_values": 2}


def counts(step):
    kind = step[0]
    return {"light": LIGHT_USES.get(kind, 0), "link": LINKS.get(kind, LINKS.get((kind, step[-1]), 0)),
            "chunk": CHUNKS[step[2]] if kind == "up" else 0, "expert": kind == "down"}


class Part:

    def __init__(self, steps, before):
        self.steps, self.before, self.each = steps, dict(before), {}
        self.ahead = dict(steps)
        run = {k: 0 for k in before}
        for step, _ in steps:
            self.each[step] = dict(run)
            for k, n in counts(step).items():
                run[k] += n
        self.total = run

    def at(self, it):
        return Place(self, it)


class Place:

    def __init__(self, part, it):
        self.part, self.it = part, it
        self.looped = not isinstance(it, int)

    def first(self, what, step):
        return self.part.before[what] + self.part.each[step][what]

    def count(self, what, n, ring=1):
        assert not self.looped or n // ring > 0
        return self.it * (self.part.total[what] // ring) + n // ring if self.looped else n // ring

    def nth(self, ahead, per, more):
        assert not self.looped or ahead * per + more > 0
        return self.it * per + (ahead * per + more)


def decoder(nc, t):
    passes = t["x"].shape[0] * S // G // STREAMS
    start = {"light": 0, "link": 0, "chunk": 2, "expert": 2}
    head, body, tail = plan()
    head = Part(head, start)
    body = Part(body, {k: start[k] + head.total[k] for k in start})
    tail = Part(tail, {k: body.before[k] + (passes - 1) * body.total[k] for k in start})
    assert all(body.total[k] % n == 0 for k, n in (("light", LIGHT), ("chunk", 2), ("expert", 2)))

    with ExitStack() as ctx:
        def sb(name, shape, dt=F32):
            return ctx.enter_context(nc.sbuf_tensor(name, shape, dt))

        def sem(name):
            return ctx.enter_context(nc.semaphore(name))

        def sems(name, n):
            return [sem(f"{name}{i}") for i in range(n)]

        def cut(tile, columns):
            out, at = {}, 0
            for name, rows, n in columns:
                out[name] = tile[0:rows, at:at + n]
                at += n
            return out

        att_pack = sb("att_pack", [P, width(ATT_PACK)])
        ffn_pack = sb("ffn_pack", [P, width(FFN_PACK)])
        mask_pack = sb("mask_pack", [P, width(MASK_PACK)], BF16)
        small = cut(att_pack, ATT_PACK) | cut(ffn_pack, FFN_PACK) | cut(mask_pack, MASK_PACK)
        ident, parity, pair_mask, vmask, outmask = (small[k] for k in ("ident", "parity", "pair_mask", "vmask", "outmask"))
        mean_w, iota, eps = (small[k] for k in ("mean_w", "iota", "eps"))
        w_attn, b_attn, w_proj, b_proj = (small[k] for k in ("w_attn", "b_attn", "w_proj", "b_proj"))
        w_xq, b_xq, w_xk, b_xk, w_xv, b_xv = (small[k] for k in ("w_xq", "b_xq", "w_xk", "b_xk", "w_xv", "b_xv"))
        identb, causal = small["identb"], small["causal"]
        b_in, b_out, w_gate, b_gate = ({st: small[f"{k}{st}"] for st in (3, 6)}
                                       for k in ("b_in", "b_out", "w_gate", "b_gate"))
        bq_masked = sb("bq_masked", [P, 2])
        att_bias = sb("att_bias", [P, D])
        w_hi = {st: sb(f"w_hi{st}", [P, E, CHUNKS[st] * P], F32R) for st in CHUNKS}
        w_lo = {st: sb(f"w_lo{st}", [P, E, CHUNKS[st] * P], F32R) for st in CHUNKS}
        w_out = {st: sb(f"w_out{st}", [P, E, CHUNKS[st], D]) for st in CHUNKS}

        def each(name, shape, dt=F32):
            return [sb(f"{name}{s}", shape, dt) for s in range(STREAMS)]

        xin = each("xin", [P, TILES, D])
        ctx_k = each("ctx_k", [CD, SEQS, S])
        ctx_l = each("ctx_l", [P, TILES, S])
        tok_i = each("tok_i", [CD, SEQS, S], I32)
        x = each("x", [P, TILES, D])
        z = each("z", [P, TILES, D])
        xT = each("xT", [P, G])
        x_hi = each("x_hi", [P, G], F32R)
        x_lo = each("x_lo", [P, G], F32R)
        gate = each("gate", [P, TILES, E])
        gate2 = each("gate2", [P, TILES, E])
        xkT = each("xkT", [P, G])
        xv = each("xv", [P, TILES, D + 2])
        probs2 = each("probs2", [P, TILES, P])
        stats = each("stats", [P, TILES, 6])
        meanvar = each("meanvar", [P, TILES, 2])
        var_eps = each("var_eps", [P, TILES])
        ln_var = each("ln_var", [P, TILES])
        rough = each("rough", [P, TILES])
        newton = each("newton", [P, 2, TILES])
        rstd = each("rstd", [P, TILES])

        q_m = sb("q_m", [P, SEQS, 2, S])
        kT = sb("kT", [P, SEQS, S])
        k_x = sb("k_x", [P, 2, 2, PAIRS, S])
        v_x = sb("v_x", [P, SEQS, TILES, VW])
        row_max = sb("row_max", [P, 2, PAIRS])
        shifted = sb("shifted", [P, 2, PAIRS, S])
        probs = shifted[:].rearrange("p r a k -> p r (a k)")
        probsT = sb("probsT", [P, 2, TILES, P])
        inv_sum = sb("inv_sum", [P, TILES, 2])
        inv_mask = sb("inv_mask", [P, PAIRS, 2])
        heads = sb("heads", [P, SEQS, D])
        x_twice = sb("x_twice", [P, SEQS, 2, S])
        headsT = x_twice[:].rearrange("p b a q -> p (b a q)").rearrange("p (a b q) -> p a b q", a=2, b=SEQS)
        tok_f = [a[:].bitcast(F32) for a in tok_i]
        ctxT = sb("ctxT", [CD, G])
        gate_src = sb("gate_src", [P, 2, TILES * S])
        picked = sb("picked", [P, E, TILES * S])
        hidden = sb("hidden", [P, 2, max(CHUNKS.values()), G])
        w_raw = hidden[:].rearrange("p m c q -> p (m c) q")
        logits = sb("logits", [P, TILES, E])
        top = sb("top", [P, TILES, 8])
        top_at = sb("top_at", [P, TILES, 8], U32)
        top_atf = sb("top_atf", [P, TILES, 2])
        top_w = sb("top_w", [P, TILES, 2])
        gap = sb("gap", [P, TILES])
        gap_exp = sb("gap_exp", [P, TILES])
        exp_1 = sb("exp_1", [P, TILES])
        mask_f32 = picked[:].rearrange("p e c -> p (e c)")[:, 0:width(MASK_PACK)]
        idle = sb("idle", [P, 1])
        idle_pool = sb("idle_pool", [P, 1])
        hit = sb("hit", [P, TILES, 2, E])
        gateT = sb("gateT", [E, TILES, P])
        max2 = sb("max2", [P, TILES])
        inv2 = sb("inv2", [P, TILES])
        xqT = [a[:] for a in xT]
        probs2T = [a[:].rearrange("p (t q) -> p t q", t=TILES) for a in xT]
        shifted2 = [a[:, 0:TILES * S].rearrange("p (t q) -> p t q", t=TILES) for a in xkT]

        light = ctx.enter_context(nc.psum_tensor("light", [P, LIGHT, 512], F32))
        hid = ctx.enter_context(nc.psum_tensor("hid", [P, 2, 512], F32))
        mix = ctx.enter_context(nc.psum_tensor("mix", [P, 2, 512], F32))

        consts_in = sem("consts_in")
        masks_in = sem("masks_in")
        masks_done = sem("masks_done")
        small_in = sem("small_in")
        w_raw_in = sems("w_raw_in", RAW)
        w_out_in = {st: sem(f"w_out_in{st}") for st in CHUNKS}
        w_hi_done = sem("w_hi_done")
        w_lo_done = sem("w_lo_done")
        x_stored = sems("x_stored", STREAMS)
        x_hi_done = sems("x_hi_done", STREAMS)
        xT_done = sems("xT_done", STREAMS)
        ln_var_done = sems("ln_var_done", STREAMS)
        is_e_done = sem("is_e_done")
        x_in = sems("x_in", STREAMS)
        ctx_in = sems("ctx_in", STREAMS)
        x_out = sems("x_out", STREAMS)
        light_full = sems("light_full", LIGHT)
        light_done = sems("light_done", LIGHT)
        hid_full = sems("hid_full", 2)
        hid_done = sems("hid_done", 2)
        mix_full = sems("mix_full", 2)
        mix_done = sems("mix_done", 2)
        cleared = sem("cleared")
        ones_set = sem("ones_set")
        act_set_up = sem("act_set_up")
        bias_full = sem("bias_full")
        bias_done = sem("bias_done")
        biased = sems("biased", STREAMS)
        k_x_done = sem("k_x_done")
        scores_read = sem("scores_read")
        exp_done = sems("exp_done", 2)
        tok_done = sem("tok_done")
        picked_done = sem("picked_done")
        gate2_done = sem("gate2_done")
        var_done = sems("var_done", STREAMS)
        rough_done = sems("rough_done", STREAMS)
        x_done = sems("x_done", STREAMS)
        gate_done = sems("gate_done", STREAMS)
        gap_done = sem("gap_done")
        gap_exp_done = sem("gap_exp_done")
        probs2_done = sem("probs2_done")
        dve_step = sem("dve_step")

        x_tiles = t["x"].rearrange("(g t b) q d -> (b q) g t d", g=passes * STREAMS, t=TILES)
        out_tiles = t["out"].rearrange("(g t b) q d -> (b q) g t d", g=passes * STREAMS, t=TILES)
        ctx_tiles = t["ctx_512"].rearrange("(g t b) k c -> (b k) g t c", g=passes * STREAMS, t=TILES)
        ctx_seqs = t["ctx_512"].rearrange("(g b) k c -> k g b c", g=passes * STREAMS)
        tok_seqs = t["tok"].rearrange("(g b) k c -> k g b c", g=passes * STREAMS)

        def piece(parts, k):
            st, a = piece_at(k)
            return parts[st][:].rearrange("p e h -> p (e h)")[:, a:a + PIECE]

        block = ctx.enter_context(nc.Block())

        @block.sync
        def _(sp):
            def load(s, group):
                sp.dma_start(xin[s][:], x_tiles[:, bass.ds(group, 1)].rearrange("p g t d -> p (g t) d")).then_inc(x_in[s], 16)
                sp.dma_start(ctx_l[s][:], ctx_tiles[:, bass.ds(group, 1)].rearrange("p g t c -> p (g t) c")).then_inc(ctx_in[s], 16)
                sp.dma_start(ctx_k[s][:], ctx_seqs[:, bass.ds(group, 1)].rearrange("p g b c -> p (g b) c")).then_inc(ctx_in[s], 16)
                sp.dma_start(tok_i[s][:], tok_seqs[:, bass.ds(group, 1)].rearrange("p g b c -> p (g b) c")).then_inc(ctx_in[s], 16)

            def store(s, group):
                sp.dma_start(out_tiles[:, bass.ds(group, 1)].rearrange("p g t d -> p (g t) d"), x[s][:]).then_inc(x_out[s], 16)

            for s in range(STREAMS):
                sp.sem_inc(x_stored[s], 1)
            for s in range(STREAMS):
                load(s, s)
            for k in range(PIECES):
                if k >= RAW:
                    sp.wait_ge(w_lo_done, k - RAW + 1)
                st, a = piece_at(k)
                sp.dma_start(w_raw[:, k % RAW], t[f"w_in{st}"].rearrange("p e h -> p (e h)")[:, a:a + PIECE]
                             ).then_inc(w_raw_in[k % RAW], 16)
            with sp.Fori(0, passes - 1) as it:
                for s in range(STREAMS):
                    sp.wait_ge(x_done[s], it * LNS + 1)
                    sp.wait_ge(x_done[s], 1)
                    load(s, it * STREAMS + (STREAMS + s))
                for s in range(STREAMS):
                    sp.wait_ge(x_done[s], it * LNS + LNS)
                    sp.wait_ge(x_done[s], LNS)
                    store(s, it * STREAMS + s)
                    sp.wait_ge(x_out[s], it * 16 + 16)
                    sp.sem_inc(x_stored[s], 1)
            for s in range(STREAMS):
                sp.wait_ge(x_done[s], passes * LNS)
                store(s, (passes - 1) * STREAMS + s)
            for s in range(STREAMS):
                sp.wait_ge(x_out[s], 16 * passes)

        @block.gpsimd
        def _(pool):
            pool.memset(v_x[:], 0.0).then_inc(cleared, 1)
            for s in range(STREAMS):
                pool.memset(xv[s][:], 1.0).then_inc(cleared, 1)
                pool.memset(probs2[s][:], 0.0).then_inc(cleared, 1)
            pool.wait_ge(cleared, CLEARED)
            for pl in range(2):
                rows = slice(S * pl, S * pl + S)
                pool.memset(v_x[rows, :, :, 4 * HD + pl], 1.0).then_inc(ones_set, 1)
                pool.wait_ge(ones_set, pl + 1)
            pool.wait_ge(consts_in, 16)

            def run(at):
                def read_out(step, more=0):
                    u = at.first("light", step) + more
                    pool.wait_ge(light_done[u % LIGHT], at.count("light", u, LIGHT) + 1)

                def full(step):
                    u = at.first("light", step)
                    pool.wait_ge(light_full[u % LIGHT], at.count("light", u, LIGHT) + 1)

                for step, ahead in at.part.steps:
                    kind, s = step[:2]
                    if kind == "w_split":
                        k = step[2]
                        pool.wait_ge(w_hi_done, k + 1)
                        pool.tensor_tensor(piece(w_lo, k), w_raw[:, k % RAW], piece(w_hi, k).bitcast(F32),
                                           ALU.subtract).then_inc(w_lo_done, 1)
                    elif kind == "att_in":
                        full(step)
                        pool.wait_ge(bias_done, 1)
                        pool.tensor_tensor(xin[s][:], xin[s][:],
                                           att_bias[:].unsqueeze(1).to_broadcast([P, TILES, D]),
                                           ALU.add).then_inc(biased[s], 1)
                    elif kind == "ctx_in":
                        read_out(step)
                        pool.tensor_tensor(idle_pool[:], eps, eps, ALU.mult)
                        for e in range(E):
                            pool.tensor_scalar(picked[:, e], gate_src[:, 1], float(e), None,
                                               ALU.is_equal).then_inc(is_e_done, 1)
                            pool.wait_ge(is_e_done, at.nth(ahead, E * STREAMS, s * E + e + 1))
                            pool.tensor_tensor(picked[:, e], picked[:, e], gate_src[:, 0],
                                               ALU.mult).then_inc(picked_done, 1)
                    elif kind == "ln_turn" and step[2] == 3:
                        full(step)
                        pool.tensor_tensor(x[s][:], x[s][:], b_xv.unsqueeze(1).to_broadcast([P, TILES, D]),
                                           ALU.add).then_inc(biased[s], 1)

            run(head.at(0))
            with pool.Fori(0, passes - 1) as it:
                run(body.at(it))
            run(tail.at(passes - 1))

        @block.scalar
        def _(act):
            for ready in hid_done:
                act.sem_inc(ready, 1)
            act.preload_act_table_set(EXP_LN_SET)
            act.dma_start(att_pack[:], t["att_pack"]).then_inc(consts_in, 16)
            act.dma_start(mask_f32, t["mask_pack"]).then_inc(masks_in, 16)
            for st in CHUNKS:
                if st == 3:
                    act.dma_start(ffn_pack[:], t["ffn_pack"]).then_inc(small_in, 16)
                act.dma_start(w_out[st][:], t[f"w_out{st}"]).then_inc(w_out_in[st], 16)
            act.wait_ge(consts_in, 16)
            for par in range(2):
                act.activation(bq_masked[:, par:par + 1], b_attn[:, 0:1], ACT.Identity,
                               scale=parity[:, par:par + 1]).then_inc(act_set_up, 1)
            act.wait_ge(act_set_up, 2)
            act.wait_ge(cleared, CLEARED)

            def run(at):
                def full(u):
                    act.wait_ge(light_full[u % LIGHT], at.count("light", u, LIGHT) + 1)

                def read_out(u):
                    act.wait_ge(light_done[u % LIGHT], at.count("light", u, LIGHT) + 1)

                def bank(u):
                    return light[:, u % LIGHT]

                for step, ahead in at.part.steps:
                    kind, s = step[:2]
                    u = at.first("light", step)
                    seqs = lambda a: a.rearrange("p (b q) -> p b q", b=SEQS)
                    tiles = lambda a: a.rearrange("p (t q) -> p t q", t=TILES)
                    if kind == "w_split":
                        k = step[2]
                        act.wait_ge(w_raw_in[k % RAW], 16 * (k // RAW) + 16)
                        act.activation(piece(w_hi, k), w_raw[:, k % RAW], ACT.Copy).then_inc(w_hi_done, 1)
                    elif kind == "set_up":
                        act.wait_ge(bias_full, 1)
                        act.activation(att_bias[:], hid[:, 1, 0:D], ACT.Copy).then_inc(bias_done, 1)
                    elif kind == "att_in":
                        full(u)
                        act.activation(xT[s][:], bank(u), ACT.Copy).then_inc(xT_done[s], 1)
                        for a in range(2):
                            ins = act.activation(x_twice[:, :, a], seqs(bank(u)), ACT.Copy)
                        ins.then_inc(light_done[u % LIGHT], 1)
                    elif kind == "att_qk":
                        full(u)
                        act.wait_ge(scores_read, at.nth(ahead, STREAMS * SEQS, s * SEQS))
                        for par in range(2):
                            ins = act.activation(q_m[:, :, par], seqs(bank(u)), ACT.Identity,
                                                 bias=bq_masked[:, par:par + 1], scale=parity[:, par:par + 1])
                        ins.then_inc(light_done[u % LIGHT], 1)
                        full(u + 1)
                        act.wait_ge(k_x_done, at.nth(ahead, STREAMS * SEQS // 2, s * SEQS // 2))
                        act.activation(kT[:], seqs(bank(u + 1)), ACT.Identity,
                                       bias=b_attn[:, 1:2]).then_inc(light_done[(u + 1) % LIGHT], 1)
                    elif kind == "ctx_in":
                        full(u + 1)
                        act.activation(ctxT[:], bank(u + 1)[0:CD], ACT.Copy).then_inc(light_done[(u + 1) % LIGHT], 1)
                    elif kind == "ctx_kv":
                        full(u)
                        act.activation(xkT[s][:], bank(u), ACT.Identity,
                                       bias=b_xk[:, 0:1]).then_inc(light_done[u % LIGHT], 1)
                        full(u + 1)
                        act.activation(xv[s][:, :, 0:D], tiles(bank(u + 1)),
                                       ACT.Copy).then_inc(light_done[(u + 1) % LIGHT], 1)
                    elif kind == "att_scores":
                        r = step[2] % 2
                        read_out(u)
                        act.activation(probs[:, r], shifted[:, r].rearrange("p a k -> p (a k)"), ACT.Exp,
                                       scale=ATT_SCALE).then_inc(exp_done[r], 1)
                    elif kind == "att_turn":
                        full(u)
                        act.activation(probsT[:, step[2] % 2], tiles(bank(u)), ACT.Copy).then_inc(light_done[u % LIGHT], 1)
                    elif kind == "att_join":
                        full(u)
                        j = step[2]
                        act.activation(headsT[:, :, 4 * j:4 * j + 4].rearrange("p a b q -> p b a q"),
                                       bank(u).rearrange("p (b a q) -> p b a q", b=4, a=2),
                                       ACT.Copy).then_inc(light_done[u % LIGHT], 1)
                    elif kind == "ln_stats":
                        n = step[2] + 1
                        act.wait_ge(var_done[s], at.nth(ahead, LNS, n))
                        act.activation(ln_var[s][:], meanvar[s][:, :, 1], ACT.Ln, bias=eps[:, 0:1]).then_inc(ln_var_done[s], 1)
                        act.wait_ge(ln_var_done[s], at.nth(ahead, LNS, n))
                        act.activation(rough[s][:], ln_var[s][:], ACT.Exp, scale=-0.5).then_inc(rough_done[s], 1)
                    elif kind == "ln_turn":
                        full(u)
                        if step[2] in WHOLE:
                            ins = act.activation(xT[s][:], bank(u), ACT.Copy)
                            if step[2] in SPLIT:
                                ins.then_inc(xT_done[s], 1)
                        if step[2] in SPLIT:
                            act.activation(x_hi[s][:], bank(u), ACT.Copy).then_inc(x_hi_done[s], 1)
                        else:
                            ins.then_inc(light_done[u % LIGHT], 1)
                    elif kind == "up":
                        stage, e = step[2:]
                        m = at.first("expert", ("down", s, stage, e))
                        for c in range(CHUNKS[stage]):
                            n = at.first("chunk", step) + c
                            act.wait_ge(hid_full[n % 2], at.count("chunk", n, 2) + 1)
                            if stage == 3 and e == c == 0:
                                act.wait_ge(small_in, 16)
                            if c == 0:
                                act.wait_ge(mix_full[m % 2], at.count("expert", m, 2))
                            k = e * CHUNKS[stage] + c
                            act.activation(hidden[:, m % 2, c], hid[:, n % 2], ACT.Relu,
                                           bias=b_in[stage][:, k:k + 1] if stage in b_in else 0.0
                                           ).then_inc(hid_done[n % 2], 1)
                    elif kind == "router" and step[2] == 6:
                        act.wait_ge(gap_done, at.nth(ahead, STREAMS, s + 1))
                        act.activation(gap_exp[:], gap[:], ACT.Exp).then_inc(gap_exp_done, 1)
                    elif kind == "gateT":
                        full(u)
                        act.activation(gateT[:], tiles(bank(u)[0:E]), ACT.Copy).then_inc(light_done[u % LIGHT], 1)
                    elif kind == "x_q":
                        full(u)
                        act.activation(xqT[s], bank(u), ACT.Identity, bias=b_xq[:, 0:1]).then_inc(light_done[u % LIGHT], 1)
                    elif kind == "x_scores":
                        read_out(u)
                        for hb in range(2):
                            rows = slice(S * hb, S * hb + S)
                            act.activation(probs2[s][rows, :, S * hb:S * hb + S], shifted2[s][rows],
                                           ACT.Exp).then_inc(probs2_done, 1)
                    elif kind == "x_turn":
                        full(u)
                        act.activation(probs2T[s], tiles(bank(u)), ACT.Copy).then_inc(light_done[u % LIGHT], 1)

            run(head.at(0))
            with act.Fori(0, passes - 1) as it:
                act.preload_act_table_set(EXP_LN_SET)
                run(body.at(it))
            run(tail.at(passes - 1))

        @block.vector
        def _(dve):
            for ready in mix_done:
                dve.sem_inc(ready, 1)
            dve.wait_ge(consts_in, 16)
            dve.wait_ge(cleared, CLEARED)
            dve.wait_ge(ones_set, 2)
            dve.wait_ge(masks_in, 16)
            dve.tensor_copy(mask_pack[:], mask_f32).then_inc(masks_done, 1)

            def run(at):
                linked = [at.part.before["link"]]

                def link(ins):
                    ins.then_inc(dve_step, 1)
                    dve.wait_ge(dve_step, at.count("link", linked[0]) + 1)
                    linked[0] += 1

                def full(u):
                    dve.wait_ge(light_full[u % LIGHT], at.count("light", u, LIGHT) + 1)
                    return light[:, u % LIGHT]

                def link_bank(u, ins):
                    ins.then_inc(light_done[u % LIGHT], 1)
                    dve.wait_ge(light_done[u % LIGHT], at.count("light", u, LIGHT) + 1)

                def carry_wait():
                    dve.memset(idle[:], 0.0)

                tiles = lambda a: a.rearrange("p (t c) -> p t c", t=TILES)
                flat = lambda a: a.rearrange("p t d -> p (t d)")
                for step, ahead in at.part.steps:
                    kind, s = step[:2]
                    u = at.first("light", step)
                    assert linked[0] == at.first("link", step), step
                    if kind == "att_keys":
                        n = step[2]
                        if n == 0:
                            u = at.first("light", ("att_qk", s)) + 1
                            dve.wait_ge(light_done[u % LIGHT], at.count("light", u, LIGHT) + 1)
                        dve.wait_ge(scores_read, at.nth(ahead, STREAMS * SEQS, s * SEQS + max(0, 2 * n - 2)))
                        for j in range(PAIRS):
                            ins = dve.tensor_scalar(k_x[:, n % 2, :, j, :], kT[:, 2 * n:2 * n + 2], pair_mask[:, j:j + 1],
                                                    None, ALU.mult)
                        ins.then_inc(k_x_done, 1)
                    elif kind == "att_v":
                        for half in range(2):
                            v = full(u + half)
                            for i in range(4):
                                ins = dve.tensor_tensor(v_x[:, 4 * half + i, :, 0:4 * HD],
                                                        tiles(v[:, i * D:(i + 1) * D]), tiles(vmask), ALU.mult)
                            ins.then_inc(light_done[(u + half) % LIGHT], 1)
                    elif kind == "ctx_in":
                        dve.wait_ge(ctx_in[s], at.nth(ahead, 48, 48))
                        dve.tensor_copy(tok_f[s], tok_i[s][:]).then_inc(tok_done, 1)
                        dve.tensor_copy(gate_src[:].rearrange("p a c -> p (a c)"),
                                        full(u)).then_inc(light_done[u % LIGHT], 1)
                    elif kind == "gates":
                        dve.wait_ge(picked_done, at.nth(ahead, E * STREAMS, (s + 1) * E))
                        dve.tensor_reduce(gate2[s][:].rearrange("p t e -> p e t"),
                                          picked[:].rearrange("p e (t k) -> p e t k", t=TILES), AX.X,
                                          ALU.add).then_inc(gate2_done, 1)
                        dve.wait_ge(gate2_done, at.nth(ahead, STREAMS, s + 1))
                    elif kind == "att_scores":
                        r = step[2] % 2
                        n = (s * SEQS + step[2]) // 2
                        sc = full(u).rearrange("p (a k) -> p a k", a=PAIRS)
                        link(dve.tensor_reduce(row_max[:, r], sc, AX.X, ALU.max))
                        dve.wait_ge(exp_done[r], at.nth(ahead, SEQS * STREAMS // 2, n))
                        dve.tensor_tensor(shifted[:, r], sc,
                                          row_max[:, r].unsqueeze(2).to_broadcast([P, PAIRS, S]),
                                          ALU.subtract).then_inc(light_done[u % LIGHT], 1)
                    elif kind == "att_values":
                        o = tiles(full(u)[:, 0:TILES * VW])
                        link(dve.reciprocal(inv_sum[:], o[:, :, 4 * HD:4 * HD + 2]))
                        link(dve.tensor_tensor(inv_mask[:],
                                               inv_sum[:].rearrange("p t a -> p (t a)").unsqueeze(2).to_broadcast([P, PAIRS, 2]),
                                               outmask.unsqueeze(1).to_broadcast([P, PAIRS, 2]), ALU.mult))
                        dve.tensor_tensor(heads[:, step[2]].rearrange("p (t c d) -> p t c d", t=TILES, d=HD),
                                          o[:, :, 0:4 * HD].rearrange("p t (c d) -> p t c d", d=HD),
                                          inv_mask[:].rearrange("p (t a) b -> p t (a b)", t=TILES).unsqueeze(3)
                                          .to_broadcast([P, TILES, 4, HD]),
                                          ALU.mult).then_inc(light_done[u % LIGHT], 1)
                    elif kind == "att_out":
                        dve.wait_ge(biased[s], at.nth(ahead, 2, 1))
                        y = full(u)
                        link_bank(u, dve.tensor_tensor(flat(z[s][:]), y, flat(xin[s][:]), ALU.add))
                    elif kind == "cummean":
                        y = full(u)
                        link_bank(u, dve.tensor_tensor(flat(z[s][:]), y, flat(x[s][:]), ALU.add))
                    elif kind == "ln_stats":
                        for i in range(TILES):
                            ins = dve.bn_stats(stats[s][:, i], z[s][:, i])
                        link(ins)
                        carry_wait()
                        for i in range(TILES):
                            ins = dve.bn_aggr(meanvar[s][:, i], stats[s][:, i])
                        ins.then_inc(var_done[s], 1)
                        dve.wait_ge(var_done[s], at.nth(ahead, LNS, step[2] + 1))
                        link(dve.tensor_scalar(var_eps[s][:], meanvar[s][:, :, 1], EPS, None, ALU.add))
                    elif kind == "ln_scale":
                        dve.wait_ge(rough_done[s], at.nth(ahead, LNS, step[2] + 1))
                        link(dve.scalar_tensor_tensor(out=newton[s][:, 0], in0=rough[s][:], scalar=-0.5, in1=rough[s][:],
                                                      op0=ALU.mult, op1=ALU.mult))
                        link(dve.tensor_tensor(newton[s][:, 1], newton[s][:, 0], var_eps[s][:], ALU.mult))
                        link(dve.scalar_tensor_tensor(out=rstd[s][:], in0=newton[s][:, 1], scalar=1.5, in1=rough[s][:],
                                                      op0=ALU.add, op1=ALU.mult))
                        if step[2] == 0:
                            dve.wait_ge(x_stored[s], at.nth(ahead, 1, 1))
                        for i in range(TILES):
                            ins = dve.tensor_scalar(x[s][:, i], z[s][:, i], meanvar[s][:, i, 0:1], rstd[s][:, i:i + 1],
                                                    ALU.subtract, ALU.mult)
                        ins.then_inc(x_done[s], 1)
                        dve.wait_ge(x_done[s], at.nth(ahead, LNS, step[2] + 1))
                    elif kind == "ln_split":
                        u = at.first("light", ("ln_turn", s, step[2]))
                        dve.wait_ge(x_hi_done[s], at.nth(ahead, len(SPLIT), SPLIT.index(step[2]) + 1))
                        dve.tensor_tensor(x_lo[s][:], full(u), x_hi[s][:].bitcast(F32),
                                          ALU.subtract).then_inc(light_done[u % LIGHT], 1)
                    elif kind == "down":
                        stage, e = step[2:]
                        m = at.first("expert", step)
                        dve.wait_ge(mix_full[m % 2], at.count("expert", m, 2) + 1)
                        if e > 0:
                            dve.wait_ge(mix_done[(m - 1) % 2], at.count("expert", m - 1, 2) + 1)
                        elif stage != 2:
                            dve.wait_ge(gate_done[s], at.nth(ahead, 2, {3: 1, 6: 2}[stage]))
                        g = gate2[s] if stage == 2 else gate[s]
                        so_far = x[s] if e == 0 else z[s]
                        for i in range(TILES):
                            ins = dve.scalar_tensor_tensor(out=z[s][:, i], in0=mix[:, m % 2, i * D:(i + 1) * D],
                                                           scalar=g[:, i, e:e + 1], in1=so_far[:, i],
                                                           op0=ALU.mult, op1=ALU.add)
                        ins.then_inc(mix_done[m % 2], 1)
                        if e == E - 1:
                            dve.wait_ge(mix_done[m % 2], at.count("expert", m, 2) + 1)
                    elif kind == "router":
                        stage = step[2]
                        dve.wait_ge(small_in, 16)
                        link_bank(u, dve.tensor_tensor(logits[:], tiles(full(u)[:, 0:TILES * E]),
                                                       b_gate[stage].unsqueeze(1).to_broadcast([P, TILES, E]), ALU.add))
                        carry_wait()
                        for i in range(TILES):
                            ins = dve.max(top[:, i], logits[:, i])
                        link(ins)
                        carry_wait()
                        for i in range(TILES):
                            ins = dve.max_index(top_at[:, i], top[:, i], logits[:, i])
                        link(ins)
                        link(dve.tensor_copy(top_atf[:], top_at[:, :, 0:2]))
                        weights = top[:, :, 0:2]
                        if stage == 6:
                            dve.tensor_tensor(gap[:], top[:, :, 1], top[:, :, 0], ALU.subtract).then_inc(gap_done, 1)
                            dve.wait_ge(gap_exp_done, at.nth(ahead, STREAMS, s + 1))
                            link(dve.tensor_scalar(exp_1[:], gap_exp[:], 1.0, None, ALU.add))
                            link(dve.reciprocal(top_w[:, :, 0], exp_1[:]))
                            link(dve.tensor_tensor(top_w[:, :, 1], gap_exp[:], top_w[:, :, 0], ALU.mult))
                            weights = top_w[:]
                        link(dve.tensor_tensor(hit[:], iota.unsqueeze(1).unsqueeze(1).to_broadcast([P, TILES, 2, E]),
                                               top_atf[:].unsqueeze(3).to_broadcast([P, TILES, 2, E]), ALU.is_equal))
                        link(dve.tensor_tensor(hit[:], hit[:], weights.unsqueeze(3).to_broadcast([P, TILES, 2, E]),
                                               ALU.mult))
                        dve.tensor_tensor(gate[s][:], hit[:, :, 0], hit[:, :, 1], ALU.add).then_inc(gate_done[s], 1)
                    elif kind == "biases":
                        m = at.first("expert", ("down", s, step[2], BIASES_AT))
                        dve.wait_ge(mix_done[m % 2], at.count("expert", m, 2) + 1)
                        y = full(u)
                        link_bank(u, dve.tensor_tensor(flat(z[s][:]), y, flat(z[s][:]), ALU.add))
                    elif kind == "x_scores":
                        sc = tiles(full(u)[:, 0:TILES * S])
                        link(dve.tensor_reduce(max2[:], sc, AX.X, ALU.max))
                        dve.tensor_tensor(shifted2[s], sc, max2[:].unsqueeze(2).to_broadcast([P, TILES, S]),
                                          ALU.subtract).then_inc(light_done[u % LIGHT], 1)
                    elif kind == "x_values":
                        dve.wait_ge(biased[s], at.nth(ahead, 2, 2))
                        for half in range(2):
                            o = full(u + half)[:, 0:2 * (D + 2)].rearrange("p (t c) -> p t c", t=2)
                            link(dve.reciprocal(inv2[:, 2 * half:2 * half + 2], o[:, :, D]))
                            for i in range(2):
                                n = 2 * half + i
                                ins = dve.scalar_tensor_tensor(out=z[s][:, n], in0=o[:, i, 0:D], scalar=inv2[:, n:n + 1],
                                                               in1=x[s][:, n], op0=ALU.mult, op1=ALU.add)
                            link_bank(u + half, ins)
                assert linked[0] == at.part.before["link"] + at.part.total["link"]

            run(head.at(0))
            with dve.Fori(0, passes - 1) as it:
                run(body.at(it))
            run(tail.at(passes - 1))

        @block.tensor
        def _(pe):
            for ready in hid_full + mix_full:
                pe.sem_inc(ready, 1)
            pe.wait_ge(consts_in, 16)
            def run(at):
                taken = [-1]

                def take(u):
                    pe.wait_ge(light_done[u % LIGHT], at.count("light", u, LIGHT))
                    taken[0] = u
                    return light[:, u % LIGHT]

                def read_out(step, more=0):
                    if at.part.ahead.get(step) != ahead:
                        return
                    u = at.first("light", step) + more
                    if u + LIGHT > taken[0]:
                        pe.wait_ge(light_done[u % LIGHT], at.count("light", u, LIGHT) + 1)

                for step, ahead in at.part.steps:
                    kind, s = step[:2]
                    u = at.first("light", step)
                    b = step[2] if len(step) > 2 else None
                    if kind == "set_up":
                        pe.matmul(hid[:, 1, 0:D], b_attn[:, 2:3].to_broadcast([P, P]), w_proj, start=True, stop=False)
                        pe.matmul(hid[:, 1, 0:D], outmask[0:1, 0:1].to_broadcast([1, P]), b_proj, start=False,
                                  stop=True).then_inc(bias_full, 1)
                        pe.wait_ge(cleared, CLEARED)
                        pe.wait_ge(ones_set, 2)
                    elif kind == "att_in":
                        bank = take(u)
                        pe.wait_ge(x_in[s], at.nth(ahead, 16, 16))
                        for i in range(TILES):
                            ins = pe.transpose(bank[:, i * P:(i + 1) * P], xin[s][:, i], ident)
                        ins.then_inc(light_full[u % LIGHT], 1)
                    elif kind == "att_qk":
                        for j in range(2):
                            bank = take(u + j)
                            if j == 0:
                                pe.wait_ge(xT_done[s], at.nth(ahead, 3, 1))
                            pe.matmul(bank, w_attn[:, j * D:(j + 1) * D], xT[s][:], start=True,
                                      stop=True).then_inc(light_full[(u + j) % LIGHT], 1)
                    elif kind == "att_v":
                        for half in range(2):
                            bank = take(u + half)
                            if half == 0:
                                read_out(("att_in", s))
                            for i in range(4):
                                ins = pe.matmul(bank[:, i * D:(i + 1) * D],
                                                x_twice[:, 4 * half + i].rearrange("p a q -> p (a q)"),
                                                w_attn[:, 2 * D:3 * D], start=True, stop=True)
                            ins.then_inc(light_full[(u + half) % LIGHT], 1)
                    elif kind == "ctx_in":
                        bank = take(u)
                        pe.wait_ge(ctx_in[s], at.nth(ahead, 48, 48))
                        pe.wait_ge(tok_done, at.nth(ahead, STREAMS, s + 1))
                        take(u + 1)
                        pe.wait_ge(masks_done, 1)
                        pe.matmul(bank[:, 0:2], identb, identb[:, 0:2], start=True, stop=True)
                        for j, src in enumerate((ctx_k[s], tok_f[s])):
                            for i in range(TILES):
                                ins = pe.transpose(bank[:, j * TILES * S + i * S:j * TILES * S + (i + 1) * S],
                                                   src[:, 2 * i:2 * i + 2].rearrange("p b c -> p (b c)"),
                                                   ident[0:CD, 0:CD])
                        ins.then_inc(light_full[u % LIGHT], 1)
                        bank = light[:, (u + 1) % LIGHT]
                        for i in range(TILES):
                            ins = pe.transpose(bank[0:CD, i * P:(i + 1) * P], ctx_l[s][:, i], ident)
                        ins.then_inc(light_full[(u + 1) % LIGHT], 1)
                    elif kind == "ctx_kv":
                        bank = take(u)
                        read_out(("ctx_in", s), 1)
                        pe.matmul(bank, w_xk, ctxT[:], start=True, stop=True).then_inc(light_full[u % LIGHT], 1)
                        bank = take(u + 1)
                        for i in range(TILES):
                            ins = pe.matmul(bank[:, i * D:(i + 1) * D], ctxT[:, i * P:(i + 1) * P], w_xv,
                                            start=True, stop=True)
                        ins.then_inc(light_full[(u + 1) % LIGHT], 1)
                    elif kind == "att_scores":
                        bank = take(u)
                        if b == 0:
                            read_out(("att_qk", s))
                        if b % 2 == 0:
                            pe.wait_ge(k_x_done, at.nth(ahead, STREAMS * SEQS // 2, s * SEQS // 2 + b // 2 + 1))
                        pe.matmul(bank, q_m[:, b].rearrange("p a q -> p (a q)"), k_x[:, b // 2 % 2, b % 2].rearrange("p a k -> p (a k)"),
                                  start=True, stop=False).then_inc(scores_read, 1)
                        pe.matmul(bank, identb, causal, start=False, stop=True).then_inc(light_full[u % LIGHT], 1)
                    elif kind == "att_turn":
                        bank = take(u)
                        pe.wait_ge(exp_done[b % 2], at.nth(ahead, SEQS * STREAMS // 2, (s * SEQS + b) // 2 + 1))
                        for i in range(TILES):
                            ins = pe.transpose(bank[:, i * P:(i + 1) * P], probs[:, b % 2, i * P:(i + 1) * P], ident)
                        ins.then_inc(light_full[u % LIGHT], 1)
                    elif kind == "att_values":
                        bank = take(u)
                        if b == 0:
                            for half in range(2):
                                read_out(("att_v", s), half)
                        read_out(("att_turn", s, b))
                        for i in range(TILES):
                            ins = pe.matmul(bank[:, i * VW:(i + 1) * VW], probsT[:, b % 2, i], v_x[:, b, i],
                                            start=True, stop=True)
                        ins.then_inc(light_full[u % LIGHT], 1)
                    elif kind == "att_join":
                        bank = take(u)
                        read_out(("att_values", s, 4 * b + 3))
                        for i in range(4):
                            ins = pe.transpose(bank[:, i * P:(i + 1) * P], heads[:, 4 * b + i], ident)
                        ins.then_inc(light_full[u % LIGHT], 1)
                    elif kind == "att_out":
                        bank = take(u)
                        for i in range(TILES):
                            if i % 2 == 0:
                                read_out(("att_join", s, i // 2))
                            for par in range(2):
                                ins = pe.matmul(bank[:, i * D:(i + 1) * D],
                                                headsT[:, par, 2 * i:2 * i + 2].rearrange("p b q -> p (b q)"), w_proj,
                                                start=(par == 0), stop=(par == 1))
                        ins.then_inc(light_full[u % LIGHT], 1)
                    elif kind == "ln_turn":
                        bank = take(u)
                        pe.wait_ge(x_done[s], at.nth(ahead, LNS, b + 1))
                        for i in range(TILES):
                            ins = pe.transpose(bank[:, i * P:(i + 1) * P], x[s][:, i], ident)
                        ins.then_inc(light_full[u % LIGHT], 1)
                    elif kind == "ln_split" and b == 0:
                        read_out(("ln_turn", s, 0))
                    elif kind == "up":
                        stage, e = step[2:]
                        if e == 0:
                            pe.wait_ge(bias_done, 1)
                            pe.wait_ge(w_lo_done, PIECES)
                            if stage != 2:
                                read_out(("ln_turn", s, {3: 1, 6: 4}[stage]))
                        for c in range(CHUNKS[stage]):
                            n = at.first("chunk", step) + c
                            cols = slice(c * P, (c + 1) * P)
                            pe.wait_ge(hid_done[n % 2], at.count("chunk", n, 2))
                            pe.matmul(hid[:, n % 2], w_hi[stage][:, e, cols], x_lo[s][:], start=True, stop=False)
                            pe.matmul(hid[:, n % 2], w_hi[stage][:, e, cols], x_hi[s][:], start=False, stop=False)
                            pe.matmul(hid[:, n % 2], w_lo[stage][:, e, cols], x_hi[s][:], start=False,
                                      stop=True).then_inc(hid_full[n % 2], 1)
                    elif kind == "down":
                        stage, e = step[2:]
                        m = at.first("expert", step)
                        pe.wait_ge(mix_done[m % 2], at.count("expert", m, 2))
                        if e == 0:
                            pe.wait_ge(w_out_in[stage], 16)
                        cs = CHUNKS[stage]
                        n = at.first("chunk", ("up", s, stage, e)) + cs - 1
                        pe.wait_ge(hid_done[n % 2], at.count("chunk", n, 2) + 1)
                        for i in range(TILES):
                            for c in range(cs):
                                ins = pe.matmul(mix[:, m % 2, i * D:(i + 1) * D],
                                                hidden[:, m % 2, c, i * P:(i + 1) * P],
                                                w_out[stage][:, e, c], start=(c == 0), stop=(c == cs - 1))
                        ins.then_inc(mix_full[m % 2], 1)
                    elif kind == "router":
                        bank = take(u)
                        pe.wait_ge(xT_done[s], at.nth(ahead, 3, {3: 2, 6: 3}[b]))
                        pe.wait_ge(small_in, 16)
                        for i in range(TILES):
                            ins = pe.matmul(bank[:, i * E:(i + 1) * E], xT[s][:, i * P:(i + 1) * P], w_gate[b],
                                            start=True, stop=True)
                        ins.then_inc(light_full[u % LIGHT], 1)
                    elif kind == "gateT":
                        bank = take(u)
                        pe.wait_ge(gate_done[s], at.nth(ahead, 2, {3: 1, 6: 2}[b]))
                        for i in range(TILES):
                            ins = pe.transpose(bank[0:E, i * P:(i + 1) * P], gate[s][:, i], ident)
                        ins.then_inc(light_full[u % LIGHT], 1)
                    elif kind == "biases":
                        bank = take(u)
                        read_out(("gateT", s, b))
                        for i in range(TILES):
                            ins = pe.matmul(bank[:, i * D:(i + 1) * D], gateT[:, i], b_out[b], start=True, stop=True)
                        ins.then_inc(light_full[u % LIGHT], 1)
                    elif kind == "cummean":
                        bank = take(u)
                        pe.wait_ge(x_done[s], at.nth(ahead, LNS, 3))
                        pe.matmul(bank, mean_w, x[s][:].rearrange("p t d -> p (t d)"), start=True,
                                  stop=True).then_inc(light_full[u % LIGHT], 1)
                    elif kind == "x_q":
                        bank = take(u)
                        read_out(("ln_turn", s, 3))
                        pe.matmul(bank, w_xq, xT[s][:], start=True, stop=True).then_inc(light_full[u % LIGHT], 1)
                    elif kind == "x_scores":
                        bank = take(u)
                        read_out(("x_q", s))
                        read_out(("ctx_kv", s))
                        for i in range(TILES):
                            for hb in range(2):
                                cols = slice(i * P + hb * S, i * P + hb * S + S)
                                ins = pe.matmul(bank[hb * S:hb * S + S, i * S:(i + 1) * S], xqT[s][:, cols],
                                                xkT[s][:, cols], start=True, stop=True)
                        ins.then_inc(light_full[u % LIGHT], 1)
                    elif kind == "x_turn":
                        bank = take(u)
                        pe.wait_ge(probs2_done, at.nth(ahead, 2 * STREAMS, 2 * (s + 1)))
                        for i in range(TILES):
                            ins = pe.transpose(bank[:, i * P:(i + 1) * P], probs2[s][:, i], ident)
                        ins.then_inc(light_full[u % LIGHT], 1)
                    elif kind == "x_values":
                        for half in range(2):
                            bank = take(u + half)
                            if half == 0:
                                read_out(("x_turn", s))
                                read_out(("ctx_kv", s), 1)
                            for i in range(2):
                                n = 2 * half + i
                                ins = pe.matmul(bank[:, i * (D + 2):(i + 1) * (D + 2)], probs2T[s][:, n], xv[s][:, n],
                                                start=True, stop=True)
                            ins.then_inc(light_full[(u + half) % LIGHT], 1)

            run(head.at(0))
            with pe.Fori(0, passes - 1) as it:
                run(body.at(it))
            run(tail.at(passes - 1))


def constants():
    import numpy as np

    p = np.arange(P)
    head = p // HD
    k = np.arange(S)
    causal = np.where(k[None, :] > (p % S)[:, None], -1e30, 0.0)
    row, col = p[:, None], p[None, :]
    same_seq = (row // S) == (col // S)
    f = lambda a: np.ascontiguousarray(a, np.float32)
    return {
        "ident": f(np.eye(P)), "identb": f(np.eye(P)), "causal": f(np.tile(causal, (1, PAIRS))),
        "parity": f((head % 2)[:, None] == np.arange(2)), "pair_mask": f((head // 2)[:, None] == np.arange(PAIRS)),
        "vmask": f((head // 2 % 2)[None, :] == (p // S)[:, None]), "outmask": f((p // S)[:, None] == np.arange(2)),
        "mean_w": f(np.where(same_seq & (row <= col), 1.0 / (col % S + 1), 0.0)),
        "iota": f(np.tile(np.arange(E), (P, 1))), "eps": f(np.full((P, 1), EPS)),
    }


def layouts(i):
    import numpy as np

    c = np.ascontiguousarray

    def second(w):
        return c(w.reshape(E, -1, P, D).transpose(2, 0, 1, 3))

    return {
        "x": i["x"], "ctx_512": i["ctx_512"], "tok": i["itok_BxS2xS_0_7"],
        "w_attn": i["L0_attn_W_attn"], "b_attn": c(i["L0_attn_b_attn"].reshape(3, D).T),
        "w_proj": i["L0_attn_W_proj"], "b_proj": i["L0_attn_b_proj"].reshape(1, D),
        "w_in2": c(i["L0_xattn_proj_in"].transpose(2, 0, 1)), "w_out2": second(i["L0_xattn_proj_out"].transpose(0, 2, 1)),
        "w_in3": c(i["L0_ffn_W1"].transpose(1, 0, 2)), "w_out3": second(i["L0_ffn_W2"]),
        "b_in3": c(i["L0_ffn_b1"].T), "b_out3": i["L0_ffn_b2"],
        "w_gate3": i["L0_ffn_W_gate"], "b_gate3": c(np.tile(i["L0_ffn_b_gate"], (P, 1))),
        "w_xq": i["L1_xattn_Wq"], "b_xq": i["L1_xattn_bq"].reshape(D, 1), "w_xk": i["L1_xattn_Wk"],
        "b_xk": i["L1_xattn_bk"].reshape(D, 1), "w_xv": i["L1_xattn_Wv"], "b_xv": c(np.tile(i["L1_xattn_bv"], (P, 1))),
        "w_in6": c(i["L1_ffn_W1"].transpose(1, 0, 2)), "w_out6": second(i["L1_ffn_W2"]),
        "b_in6": c(i["L1_ffn_b1"].reshape(E, CHUNKS[6], P).transpose(2, 0, 1).reshape(P, -1)), "b_out6": i["L1_ffn_b2"],
        "w_gate6": i["L1_ffn_W_router"], "b_gate6": c(np.tile(i["L1_ffn_b_router"], (P, 1))),
    }


def pack(columns):
    import numpy as np

    out = np.zeros((P, sum(n for _, n in columns)), columns[0][0].dtype)
    at = 0
    for a, n in columns:
        out[:a.shape[0], at:at + n] = a
        at += n
    return out


def kernel(**inputs):
    import numpy as np
    import concourse.bacc as bacc
    from concourse import mybir as _mybir
    from concourse.bass_utils import run_bass_kernel_spmd

    nc = bacc.Bacc("TRN2", target_bir_lowering=False, num_devices=1)
    parts = layouts({k: np.asarray(v) for k, v in inputs.items()}) | constants()
    packs = {"att_pack": ATT_PACK, "ffn_pack": FFN_PACK, "mask_pack": MASK_PACK}
    packed = {k: pack([(parts.pop(name), n) for name, _, n in columns]) for k, columns in packs.items()}
    arrays = {k: np.ascontiguousarray(v) for k, v in (parts | packed).items()}
    handles = {k: nc.dram_tensor(f"in_{k}", a.shape, _mybir.dt.from_np(a.dtype), kind="ExternalInput").ap()
               for k, a in arrays.items()}
    handles["out"] = nc.dram_tensor("out_dram", arrays["x"].shape, _mybir.dt.float32, kind="ExternalOutput").ap()
    decoder(nc, handles)
    r = run_bass_kernel_spmd(nc, [{f"in_{k}": a for k, a in arrays.items()}], core_ids=[0])
    return r.results[0]["out_dram"]
```
